# Optimizing a Trainium2 kernel written in Bass

```python
import numpy as np
import jax
import jax.numpy as jnp

def _softmax(x, axis=-1):
    return jax.nn.softmax(x, axis=axis)

def _gelu(x):
    return jax.nn.gelu(x, approximate=True)

def _silu(x):
    return jax.nn.silu(x)

def _sigmoid(x):
    return jax.nn.sigmoid(x)

def _layernorm(x, axis=-1, eps=1e-05):
    m = jnp.mean(x, axis=axis, keepdims=True)
    v = jnp.var(x, axis=axis, keepdims=True)
    return (x - m) / jnp.sqrt(v + eps)

def _scatter_add(tgt, idx, src, axis=0):
    return tgt.at[idx].add(src)

def _segment_sum(src, seg, n):
    return jax.ops.segment_sum(src, seg, n)
kernel_name = 'mk_gnn_resnorm_d4_gnn_r8_4f9fca'

def setup_inputs(seed: int=0):
    np.random.seed(seed)
    _w = jnp.asarray

    def _rec_inputs():
        import jax
        import jax.numpy as jnp
        _gk = jax.random.key(seed)
        x = -0.000202 + 1 * jax.random.normal(jax.random.fold_in(_gk, 1), (12500, 64), jnp.float32)
        _s = jax.random.randint(jax.random.fold_in(_gk, 2), (200000,), 0, 12500, jnp.int32)
        _d = jax.random.randint(jax.random.fold_in(_gk, 3), (200000,), 0, 12500, jnp.int32)
        _loop = jnp.arange(12500, dtype=jnp.int32)
        src = jnp.concatenate([_s, _d, _loop])
        dst = jnp.concatenate([_d, _s, _loop])
        _o = jnp.argsort(dst, stable=True)
        src = src[_o]
        dst = dst[_o]
        edge_attr_64 = -8.16379e-05 + 0.999858 * jax.random.normal(jax.random.fold_in(_gk, 12), (412500, 64), jnp.float32)
        edge_weight = jax.random.uniform(jax.random.fold_in(_gk, 14), (412500,), jnp.float32, 0.0, 0.999999)
        return (x, src, dst, edge_attr_64, edge_weight)
    x, src, dst, edge_attr_64, edge_weight = _rec_inputs()

    def _L0_gnn_setup():
        import jax, jax.numpy as jnp
        import numpy as np
        N_NODES = 12500
        N_EDGES = 200000
        F_DIM = 64
        key = jax.random.key(seed)
        k1, k2, k3 = jax.random.split(key, 3)
        x = jax.random.normal(k1, (N_NODES, F_DIM), dtype=jnp.float32)
        edge_index = jax.random.randint(k2, (2, N_EDGES), 0, N_NODES, dtype=jnp.int64)
        edge_weight = jax.random.uniform(k3, (N_EDGES,), dtype=jnp.float32)
        return {'x': x, 'edge_index': edge_index, 'edge_weight': edge_weight, 'num_nodes': N_NODES}
    _L0_gnn_all = _L0_gnn_setup()
    _L0_gnn_in = {k: v for k, v in _L0_gnn_all.items() if k in ()}
    del _L0_gnn_all

    def _L1_gnn_setup():
        import jax, jax.numpy as jnp
        import numpy as np
        N_NODES = 12500
        N_EDGES = 200000
        F_IN = 64
        F_HID = 16

        def _gcn_conv(x, W, b, src, dst, n):
            ones = jnp.ones(src.shape[0], x.dtype)
            deg = jax.ops.segment_sum(ones, dst, num_segments=n)
            dinv = jax.lax.rsqrt(deg)
            norm = dinv[src] * dinv[dst]
            h = x @ W
            msg = h[src] * norm[:, None]
            out = jax.ops.segment_sum(msg, dst, num_segments=n)
            return out + b
        key = jax.random.key(seed)
        k1, k2, k3, k4 = jax.random.split(key, 4)
        x = jax.random.normal(k1, (N_NODES, F_IN), dtype=jnp.float32)
        edge_index = jax.random.randint(k2, (2, N_EDGES), 0, N_NODES, dtype=jnp.int64)
        W1 = jax.random.normal(k3, (F_IN, F_HID), dtype=jnp.float32) * (1.0 / np.sqrt(F_IN))
        W2 = jax.random.normal(k4, (F_HID, F_IN), dtype=jnp.float32) * (1.0 / np.sqrt(F_HID))
        b1 = jnp.zeros((F_HID,), jnp.float32)
        b2 = jnp.zeros((F_IN,), jnp.float32)
        return {'x': x, 'edge_index': edge_index, 'W1': W1, 'b1': b1, 'W2': W2, 'b2': b2}
    _L1_gnn_all = _L1_gnn_setup()
    _L1_gnn_in = {k: v for k, v in _L1_gnn_all.items() if k in ('W1', 'b1', 'W2', 'b2')}
    del _L1_gnn_all

    def _L2_gnn_setup():
        import jax, jax.numpy as jnp
        import numpy as np
        N_NODES = 12500
        N_EDGES = 200000
        IN_SIZE = 64
        OUT_SIZE = 64
        N_HEADS = 2
        NEG_SLOPE = 0.2
        BN_EPS = 1e-05
        key = jax.random.key(seed)
        ks = jax.random.split(key, 8)
        atom = jax.random.normal(ks[0], (N_NODES, IN_SIZE), dtype=jnp.float32)
        bond = jax.random.normal(ks[1], (N_EDGES, IN_SIZE), dtype=jnp.float32)
        W = jax.random.normal(ks[2], (IN_SIZE, OUT_SIZE * N_HEADS), dtype=jnp.float32) * 0.1
        attn_l = jax.random.normal(ks[3], (N_HEADS, OUT_SIZE), dtype=jnp.float32) * 0.1
        attn_r = jax.random.normal(ks[4], (N_HEADS, OUT_SIZE), dtype=jnp.float32) * 0.1
        bn_gamma = jnp.ones((OUT_SIZE,), dtype=jnp.float32)
        bn_beta = jnp.zeros((OUT_SIZE,), dtype=jnp.float32)
        src = jax.random.randint(ks[5], (N_EDGES,), 0, N_NODES, dtype=jnp.int32)
        dst = jax.random.randint(ks[6], (N_EDGES,), 0, N_NODES, dtype=jnp.int32)
        return {'atom': atom, 'bond': bond, 'W': W, 'attn_l': attn_l, 'attn_r': attn_r, 'bn_gamma': bn_gamma, 'bn_beta': bn_beta, 'src': src, 'dst': dst}
    _L2_gnn_all = _L2_gnn_setup()
    _L2_gnn_in = {k: v for k, v in _L2_gnn_all.items() if k in ('W', 'attn_l', 'attn_r', 'bn_gamma', 'bn_beta')}
    del _L2_gnn_all

    def _L3_gnn_setup():
        import jax, jax.numpy as jnp
        import numpy as np
        N_NODES = 6250
        N_EDGES = 100000
        D_FEAT = 64
        EPS_NORM = 1e-12
        EPS_SOFTMAX = 1e-16
        key = jax.random.key(seed)
        k1, k2, k3, k4 = jax.random.split(key, 4)
        x = jax.random.normal(k1, (N_NODES, D_FEAT), dtype=jnp.float32)
        row = jax.random.randint(k2, (N_EDGES,), 0, N_NODES)
        col = jax.random.randint(k3, (N_EDGES,), 0, N_NODES)
        col = jnp.where(col == row, (col + 1) % N_NODES, col)
        edge_index = jnp.stack([row, col]).astype(jnp.int64)
        edge_attr = jax.random.uniform(k4, (N_EDGES,), dtype=jnp.float32)
        beta = jnp.ones((1,), dtype=jnp.float32)
        eps = jnp.zeros((1,), dtype=jnp.float32)
        return {'x': x, 'edge_attr': edge_attr, 'beta': beta, 'eps': eps, 'edge_index': edge_index}
    _L3_gnn_all = _L3_gnn_setup()
    _L3_gnn_in = {k: v for k, v in _L3_gnn_all.items() if k in ('beta', 'eps')}
    del _L3_gnn_all
    return {'x': x, 'src': src, 'dst': dst, 'edge_attr_64': edge_attr_64, 'edge_weight': edge_weight, 'L1_gnn_W1': _L1_gnn_in['W1'], 'L1_gnn_b1': _L1_gnn_in['b1'], 'L1_gnn_W2': _L1_gnn_in['W2'], 'L1_gnn_b2': _L1_gnn_in['b2'], 'L2_gnn_W': _L2_gnn_in['W'], 'L2_gnn_attn_l': _L2_gnn_in['attn_l'], 'L2_gnn_attn_r': _L2_gnn_in['attn_r'], 'L2_gnn_bn_gamma': _L2_gnn_in['bn_gamma'], 'L2_gnn_bn_beta': _L2_gnn_in['bn_beta'], 'L3_gnn_beta': _L3_gnn_in['beta'], 'L3_gnn_eps': _L3_gnn_in['eps']}

def reference(x, src, dst, edge_attr_64, edge_weight, L1_gnn_W1, L1_gnn_b1, L1_gnn_W2, L1_gnn_b2, L2_gnn_W, L2_gnn_attn_l, L2_gnn_attn_r, L2_gnn_bn_gamma, L2_gnn_bn_beta, L3_gnn_beta, L3_gnn_eps):
    import jax
    import jax.numpy as jnp

    def _L0_gnn_ref(x, edge_index, edge_weight, num_nodes):
        import jax, jax.numpy as jnp
        import numpy as np
        N_NODES = 12500
        N_EDGES = 200000
        F_DIM = 64
        src, dst = (edge_index[0], edge_index[1])
        msgs = x[src] * edge_weight[:, None]
        out = jax.ops.segment_sum(msgs, dst, num_segments=num_nodes)
        return out

    def _L1_gnn_ref(x, edge_index, W1, b1, W2, b2):
        import jax, jax.numpy as jnp
        import numpy as np
        N_NODES = 12500
        N_EDGES = 200000
        F_IN = 64
        F_HID = 16

        def _gcn_conv(x, W, b, src, dst, n):
            ones = jnp.ones(src.shape[0], x.dtype)
            deg = jax.ops.segment_sum(ones, dst, num_segments=n)
            dinv = jax.lax.rsqrt(deg)
            norm = dinv[src] * dinv[dst]
            h = x @ W
            msg = h[src] * norm[:, None]
            out = jax.ops.segment_sum(msg, dst, num_segments=n)
            return out + b
        n = x.shape[0]
        loops = jnp.arange(n, dtype=edge_index.dtype)
        src = jnp.concatenate([edge_index[0], loops])
        dst = jnp.concatenate([edge_index[1], loops])
        z = _gcn_conv(x, W1, b1, src, dst, n)
        recon = _gcn_conv(z, W2, b2, src, dst, n)
        return recon

    def _L2_gnn_ref(atom, bond, W, attn_l, attn_r, bn_gamma, bn_beta, src, dst):
        import jax, jax.numpy as jnp
        import numpy as np
        N_NODES = 12500
        N_EDGES = 200000
        IN_SIZE = 64
        OUT_SIZE = 64
        N_HEADS = 2
        NEG_SLOPE = 0.2
        BN_EPS = 1e-05
        N = atom.shape[0]
        H, D = attn_l.shape
        h_edge = ((atom[src] + bond) @ W).reshape(-1, H, D)
        h_node = (atom @ W).reshape(-1, H, D)
        el = jnp.einsum('ehd,hd->eh', h_edge, attn_l)
        er = jnp.einsum('nhd,hd->nh', h_node, attn_r)
        s = el + er[dst]
        s = jnp.where(s > 0, s, NEG_SLOPE * s)
        smax = jax.ops.segment_max(s, dst, num_segments=N)
        ex = jnp.exp(s - smax[dst])
        denom = jax.ops.segment_sum(ex, dst, num_segments=N)
        alpha = ex / denom[dst]
        ft = jax.ops.segment_sum(h_edge * alpha[..., None], dst, num_segments=N)
        h = ft.mean(axis=1)
        mu = h.mean(axis=0)
        var = h.var(axis=0)
        h = (h - mu) / jnp.sqrt(var + BN_EPS) * bn_gamma + bn_beta
        h = jax.nn.relu(h)
        return h

    def _L3_gnn_ref(x, edge_attr, beta, eps, edge_index):
        import jax, jax.numpy as jnp
        import numpy as np
        N_NODES = 6250
        N_EDGES = 100000
        D_FEAT = 64
        EPS_NORM = 1e-12
        EPS_SOFTMAX = 1e-16
        N, d = x.shape
        row, col = (edge_index[0], edge_index[1])
        sq = jax.ops.segment_sum(edge_attr * edge_attr, row, num_segments=N)
        ea = edge_attr / jnp.maximum(jnp.sqrt(sq), EPS_NORM)[row]
        loop = jnp.arange(N)
        row_f = jnp.concatenate([row, loop])
        col_f = jnp.concatenate([col, loop])
        ea_f = jnp.concatenate([ea, jnp.ones((N,), ea.dtype)])
        xn = x / jnp.maximum(jnp.linalg.norm(x, axis=-1, keepdims=True), EPS_NORM)
        alpha = beta[0] * ea_f
        amax = jax.ops.segment_max(alpha, row_f, num_segments=N)
        ex = jnp.exp(alpha - amax[row_f])
        denom = jax.ops.segment_sum(ex, row_f, num_segments=N)
        a = ex / (denom[row_f] + EPS_SOFTMAX)
        out = jax.ops.segment_sum(a[:, None] * xn[col_f], row_f, num_segments=N)
        return (1.0 + eps[0]) * xn + out
    edge_index = jnp.stack([src, dst])
    x = _layernorm(x + _L0_gnn_ref(x, edge_index, edge_weight, 12500), axis=-1)
    x = _layernorm(x + _L1_gnn_ref(x, edge_index, L1_gnn_W1, L1_gnn_b1, L1_gnn_W2, L1_gnn_b2), axis=-1)
    x = _layernorm(x + _L2_gnn_ref(x, edge_attr_64, L2_gnn_W, L2_gnn_attn_l, L2_gnn_attn_r, L2_gnn_bn_gamma, L2_gnn_bn_beta, src, dst), axis=-1)
    x = _layernorm(x + _L3_gnn_ref(x, edge_weight, L3_gnn_beta, L3_gnn_eps, edge_index), axis=-1)
    return x

_drawn_inputs = setup_inputs


def setup_inputs(seed=0):
    import zlib

    import numpy as np

    out = dict(_drawn_inputs(seed))
    spreads = {'L1_gnn_b1': (0.0, 0.1),
     'L1_gnn_b2': (0.0, 0.1),
     'L2_gnn_bn_gamma': (1.0, 0.2),
     'L2_gnn_bn_beta': (0.0, 0.1)}
    factors = {}
    for name, (base, spread) in spreads.items():
        noise = np.random.default_rng([zlib.crc32(name.encode()), seed]).standard_normal(out[name].shape)
        drawn = base * np.exp(spread * noise) if base else spread * noise
        out[name] = jnp.asarray(drawn.astype(out[name].dtype))
    for name, factor in factors.items():
        out[name] = (out[name] * factor).astype(out[name].dtype)
    return out
```

```python
from contextlib import ExitStack

import concourse.bass as bass
from concourse import mybir

F32 = mybir.dt.float32
I32 = mybir.dt.int32
I16 = mybir.dt.int16
U32 = mybir.dt.uint32
ALU = mybir.AluOpType
ACT = mybir.ActivationFunctionType
AX = mybir.AxisListType

P = 128
F = 64
FX = F + 1
H = 16
CHUNK = 8
BODY = 32
GROUP = 4
RING = 16
SUMS = 8
TABLES = 8
BIG = 1.0e30


def sizes(n_nodes, n_edges):
    tiles = -(-n_edges // P)
    blocks = -(-n_nodes // P)
    steps = -(-(tiles + blocks - 1) // P) * P
    return tiles, blocks, steps


class Chain:

    def __init__(self, engine, done, start):
        self.engine, self.done, self.count = engine, done, start

    def __call__(self, instruction):
        self.count += 1
        instruction.then_inc(self.done, 1)
        self.engine.wait_ge(self.done, self.count)


class Tables:
    pass


class Semaphores:
    pass


class Reached:
    loaded = stored = vec = vec2 = act = pe = pool = idx = proj = batch = 0


def build(nc, x, src, dst, edge_attr, ew, W1, b1, W2, b2, W, attn_l, attn_r, gamma, bn_beta, beta, eps, out):
    N = out.shape[0]
    NB = x.shape[0] // P
    S = src.shape[0]
    T = edge_attr.shape[0] // P
    NJ = S // P
    ITS = S // BODY
    TABLE_CUTS = min(c for c in range(1, NB + 2) if (NB + 1) % c == 0 and (NB + 1) // c * FX <= CHUNK * P)
    NPX = (NB + 1) * P

    def dram(name, shape, dt=F32):
        return nc.dram_tensor(name, shape, dt).ap()

    d = Tables()
    d.tile_ends = dram("tile_ends", [S])
    d.block_of = dram("block_of", [S], I32)
    d.tile_of = dram("tile_of", [S], I32)
    d.lane = dram("lane", [S * P + 2])
    d.src_rows = dram("src_rows", [S, P])
    d.hop1 = dram("hop1", [NB * P, H])
    d.hop2 = dram("hop2", [NB * P, H])
    d.nodes2 = dram("nodes2", [NB * P, FX])
    d.summed_edges = dram("summed_edges", [P, S * FX])
    d.scores = dram("scores", [2, S, P])
    d.weights = dram("weights", [2, S, P])
    d.scattered = [dram(f"scattered{k}", [NPX, FX]) for k in range(TABLES)]
    lane_rows = d.lane[1:1 + S * P].rearrange("(s e) -> s e", e=P)

    ctx = ExitStack()
    with ctx:
        def sb(name, shape, dt=F32):
            return ctx.enter_context(nc.sbuf_tensor(name, shape, dt))

        def sem(name):
            return ctx.enter_context(nc.semaphore(name))

        lanes_free = sb("lanes_free", [P, P])
        lane_id = sb("lane_id", [P, 1])
        earlier = sb("earlier", [P, P])
        ident = sb("ident", [P, P])
        ones = sb("ones", [P, P])
        int_tmp = sb("int_tmp", [P, P], I32)
        xcur = sb("xcur", [P, NB, FX])
        acc = sb("acc", [P, NB, 2 * FX])
        lane_col = sb("lane_col", [P, S + BODY], I16)
        src_col = sb("src_col", [P, S + BODY], I16)
        w_col = sb("w_col", [P, S])
        scatter_col = sb("scatter_col", [P, S + BODY], I16)
        scratch = sb("scratch", [P, 3 * S])
        walk_sb = sb("walk_sb", [P // 2, S], I32)
        idx = sb("idx", [P, BODY], U32)
        rows = sb("rows", [P, RING, FX])
        side = sb("side", [P, RING, FX])
        onehot = sb("onehot", [P, 2 * GROUP, P])
        onehot2 = sb("onehot2", [P, 2 * GROUP, P])
        bcast = sb("bcast", [P, 2, 2 * GROUP * P])
        bcast2 = sb("bcast2", [P, 2, 2 * GROUP * P])
        col = sb("col", [P, 6, NB])
        dinv = sb("dinv", [P, NB])
        inv_norm = sb("inv_norm", [P, NB])
        er = sb("er", [P, NB, 2])
        steps_tmp = sb("steps_tmp", [P, 8, max(NJ, 2)])
        steps_int = sb("steps_int", [P, 3, NJ], I32)
        w1_sb = sb("w1_sb", [F, H])
        w2_sb = sb("w2_sb", [H, F])
        w_heads = sb("w_heads", [P, F])
        v_rows = sb("v_rows", [P, 4, F])
        b1_sb = sb("b1_sb", [P, H])
        b2_sb = sb("b2_sb", [P, F])
        bn_sb = sb("bn_sb", [P, 6, F])
        pars = sb("pars", [P, 8])
        one_dup = sb("one_dup", [P, P])
        mask = sb("mask", [P, 1])
        dots = sb("dots", [P, GROUP, 2, F])
        dot_sums = sb("dot_sums", [P, GROUP, 2])
        carry_out = sb("carry_out", [P, 4])
        edge_val = sb("edge_val", [P, 6, 1])
        zeros = sb("zeros", [P, P])

        hist_lo = onehot2
        hist_hi = bcast[:, :, :].rearrange("p a b -> p (a b)")[:, 0:2 * GROUP * NB].rearrange("p (s n) -> p s n", n=NB)
        bcast2_flat = bcast2[:, :, :].rearrange("p a b -> p (a b)")
        pair = bcast2_flat[:, 0:2 * GROUP * 2 * FX].rearrange("p (s f) -> p s f", s=2 * GROUP)
        proj_in, proj_tr = bcast2_flat[:, 0:7 * P], bcast2_flat[:, 7 * P:14 * P]
        carry = bcast2_flat[0:1, 0:6 * P].rearrange("o (c p) -> o c p", c=6)
        carry_in = bcast2_flat[0:1, 6 * P:6 * P + 4 * (P + 1)].rearrange("o (c p) -> o c p", c=4)
        clear = bcast[:, 0, 0:(NB + 1) * FX // TABLE_CUTS]
        w_full = bcast2_flat[0:F, 0:2 * F]
        attn_sb = bcast2_flat[0:F, 2 * F:6 * F].rearrange("k (a d) -> k a d", a=2)
        attn_prod = bcast2_flat[0:F, 6 * F:10 * F].rearrange("k (c d) -> k c d", c=4)
        attn_vb = bcast2_flat[0:F, 10 * F:18 * F].rearrange("k (c p) -> k c p", c=4)
        attn_v = edge_val[0:F, 0:4, 0]
        acc_flat = acc[:, :, :].rearrange("p b f -> p (b f)")

        sums = ctx.enter_context(nc.psum_tensor("sums", [P, SUMS, 256], F32))
        pa = ctx.enter_context(nc.psum_tensor("pa", [P, 1024], F32))
        pb = ctx.enter_context(nc.psum_tensor("pb", [P, 512], F32))
        hist = ctx.enter_context(nc.psum_tensor("hist", [P, 512], F32))

        s = Semaphores()
        s.loaded = sem("loaded")
        s.stored = sem("stored")
        s.vec = sem("vec")
        s.act = sem("act")
        s.pe = sem("pe")
        s.pool = sem("pool")
        s.tiles_in = sem("tiles_in")
        s.gathered = [sem(f"gathered{q}") for q in range(RING // GROUP)]
        s.idx_filled = sem("idx_filled")
        s.weighted = sem("weighted")
        s.matmuls = sem("matmuls")
        s.onehots = sem("onehots")
        s.adds = sem("adds")
        s.hist_ready = sem("hist_ready")
        s.hist_used = sem("hist_used")
        s.src_loaded = [sem(f"src_loaded{h}") for h in range(2)]
        s.dup_counted = sem("dup_counted")
        s.lane_loaded = [sem(f"lane_loaded{h}") for h in range(2)]
        s.bond_loaded = [sem(f"bond_loaded{q}") for q in range(RING // GROUP)]
        s.edge_sums = sem("edge_sums")
        s.er_ready = sem("er_ready")
        s.lane_onehots = sem("lane_onehots")
        s.scored = sem("scored")
        s.spilled = [sem(f"spilled{h}") for h in range(2)]
        s.reloaded = [sem(f"reloaded{h}") for h in range(2)]
        s.scaled = sem("scaled")
        s.equal_ready = sem("equal_ready")
        s.spread = sem("spread")
        s.values_ready = sem("values_ready")
        s.merged = sem("merged")
        s.merged_out = sem("merged_out")
        s.scatter_done = [sem(f"scatter_done{k}") for k in range(TABLES)]
        s.batch_t = sem("batch_t")
        s.batch_copied = sem("batch_copied")
        s.proj_in = sem("proj_in_ready")
        s.proj_t = sem("proj_t")
        s.proj_copied = sem("proj_copied")
        s.proj_mm = sem("proj_mm")
        s.finish_used = sem("finish_used")
        s.finish_in = [sem(f"finish_in{h}") for h in range(2)]
        s.proj_out = sem("proj_out")
        n = Reached()

        def load(eng, to, of, slow=False):
            n.loaded += 16
            eng.dma_start(to, of, allow_slow_non_contiguous=slow).then_inc(s.loaded, 16)

        def chain(eng, name):
            return {"vec": Chain(eng, s.vec, n.vec), "act": Chain(eng, s.act, n.act),
                    "pe": Chain(eng, s.pe, n.pe), "pool": Chain(eng, s.pool, n.pool)}[name]

        def bc(ap, shape):
            return ap.to_broadcast(shape)

        def all_lanes(ap, width):
            return ap.unsqueeze(2).to_broadcast([P, NB, width])

        def constants():
            with nc.Block() as block:
                @block.sync
                def _(sp):
                    load(sp, xcur[:, :, 0:F], x.rearrange("(b p) f -> p b f", p=P))
                    load(sp, w1_sb[:, :], W1)
                    load(sp, w2_sb[:, :], W2)
                    load(sp, w_full[:, :], W)
                    load(sp, w_heads[0:F, :], W[:, 0:F])
                    load(sp, w_heads[F:P, :], W[:, F:2 * F])
                    load(sp, attn_sb[:, 0, :], attn_l.rearrange("h d -> (h d)").partition_broadcast(F))
                    load(sp, attn_sb[:, 1, :], attn_r.rearrange("h d -> (h d)").partition_broadcast(F))
                    load(sp, b1_sb[:, :], b1.partition_broadcast(P))
                    load(sp, b2_sb[:, :], b2.partition_broadcast(P))
                    load(sp, bn_sb[:, 0, :], gamma.partition_broadcast(P))
                    load(sp, bn_sb[:, 1, :], bn_beta.partition_broadcast(P))
                    load(sp, pars[:, 0:1], beta.partition_broadcast(P))
                    load(sp, pars[:, 1:2], eps.partition_broadcast(P))
                    load(sp, steps_int[:, 0, :], dst[:, P - 1:P].rearrange("(p j) e -> p (j e)", j=NJ), slow=True)
                    sp.wait_ge(s.loaded, n.loaded)

                @block.gpsimd
                def _(pool):
                    run = chain(pool, "pool")
                    run(nc.gpsimd.iota(int_tmp[:, :], [[1, P]], base=0, channel_multiplier=0))
                    run(nc.gpsimd.tensor_copy(lanes_free[:, :], int_tmp[:, :]))
                    run(nc.gpsimd.iota(int_tmp[:, 0:1], [[1, 1]], base=0, channel_multiplier=1))
                    run(nc.gpsimd.tensor_copy(lane_id[:, :], int_tmp[:, 0:1]))
                    run(nc.gpsimd.iota(int_tmp[:, 0:NJ], [[1, NJ]], base=0, channel_multiplier=NJ))
                    run(nc.gpsimd.tensor_copy(steps_tmp[:, 0, 0:NJ], int_tmp[:, 0:NJ]))
                    run(nc.gpsimd.iota(int_tmp[:, 0:NJ], [[P, NJ]], base=0, channel_multiplier=1))
                    run(nc.gpsimd.tensor_copy(steps_tmp[:, 1, 0:NJ], int_tmp[:, 0:NJ]))
                    n.pool = run.count

                @block.vector
                def _(dve):
                    run = chain(dve, "vec")
                    dve.sem_inc(s.proj_out, 1)
                    run(nc.vector.memset(ones[:, :], 1.0))
                    run(nc.vector.memset(acc[:, :, :], 0.0))
                    run(nc.vector.memset(side[:, :, F:FX], 1.0))
                    run(nc.vector.memset(xcur[:, :, F:FX], 1.0))
                    run(nc.vector.memset(zeros[:, :], 0.0))
                    dve.wait_ge(s.pool, n.pool)
                    run(nc.vector.tensor_scalar(ident[:, :], lanes_free[:, :], lane_id[:, 0:1], None, ALU.is_equal))
                    run(nc.vector.tensor_scalar(earlier[:, :], lanes_free[:, :], lane_id[:, 0:1], None, ALU.is_lt))
                    dve.wait_ge(s.loaded, n.loaded)
                    run(nc.vector.tensor_scalar(pars[:, 5:6], pars[:, 0:1], -1.0, None, ALU.mult))
                    run(nc.vector.tensor_tensor(pars[:, 2:3], pars[:, 0:1], pars[:, 5:6], ALU.max))
                    run(nc.vector.tensor_scalar(pars[:, 5:6], pars[:, 2:3], -1.0, None, ALU.mult))
                    run(nc.vector.tensor_tensor(pars[:, 3:4], pars[:, 0:1], pars[:, 5:6], ALU.add))
                    run(nc.vector.tensor_scalar(pars[:, 4:5], pars[:, 1:2], 1.0, None, ALU.add))
                    run(nc.vector.tensor_scalar(w_heads[:, :], w_heads[:, :], 0.5, None, ALU.mult))
                    for side_ in range(2):
                        run(nc.vector.tensor_tensor(
                            attn_prod[:, 2 * side_:2 * side_ + 2, :].rearrange("k c d -> k (c d)"),
                            w_full[:, :], attn_sb[:, side_, :], ALU.mult))
                    run(nc.vector.tensor_reduce(attn_v, attn_prod[:, :, :], AX.X, ALU.add))
                    run(nc.vector.tensor_copy(attn_vb, attn_v.unsqueeze(2).to_broadcast([F, 4, P])))
                    n.vec = run.count

                @block.tensor
                def _(pe):
                    run = chain(pe, "pe")
                    pe.sem_inc(s.proj_t, 1)
                    pe.wait_ge(s.vec, n.vec)
                    for c in range(4):
                        run(nc.tensor.matmul(pb[:, F * c:F * c + F], attn_vb[:, c, :], ident[0:F, 0:F],
                                             start=True, stop=True))
                    n.pe = run.count

                @block.scalar
                def _(act):
                    run = chain(act, "act")
                    act.wait_ge(s.vec, n.vec)
                    run(nc.scalar.activation(pars[:, 3:4], pars[:, 3:4], ACT.Exp))
                    act.wait_ge(s.pe, n.pe)
                    run(nc.scalar.copy(v_rows[:, :, :].rearrange("p c f -> p (c f)"), pb[:, 0:4 * F]))
                    n.act = run.count

        def walk():
            qb = acc_flat[:, 0:S]
            junk = acc_flat[:, S:2 * S]
            src_i = scratch[:, 0:S].bitcast(I32)
            dst_i = scratch[:, S:2 * S].bitcast(I32)
            with nc.Block() as block:
                @block.vector
                def _(dve):
                    run = chain(dve, "vec")
                    run(nc.vector.tensor_scalar(steps_int[:, 1, :], steps_int[:, 0, :], 7, None, ALU.arith_shift_right))
                    run(nc.vector.tensor_copy(steps_tmp[:, 2, 0:NJ], steps_int[:, 1, :]))
                    run(nc.vector.tensor_tensor(steps_tmp[:, 3, 0:NJ], steps_tmp[:, 2, 0:NJ], steps_tmp[:, 0, 0:NJ],
                                                ALU.add))
                    n.vec = run.count

                @block.sync
                def _(sp):
                    sp.wait_ge(s.vec, n.vec)
                    load(sp, d.tile_ends.rearrange("(p j) -> p j", j=NJ), steps_tmp[:, 3, 0:NJ])
                    sp.wait_ge(s.loaded, n.loaded)
                    load(sp, qb, d.tile_ends.partition_broadcast(P))
                    sp.wait_ge(s.loaded, n.loaded)
            with nc.Block() as block:
                @block.vector
                def _(dve):
                    run = chain(dve, "vec")
                    for j in range(NJ):
                        run(nc.vector.tensor_scalar(junk, qb, steps_tmp[:, 1, j:j + 1], 0.0, ALU.is_lt, ALU.add,
                                                    accum_out=steps_tmp[:, 4, j:j + 1]))
                    run(nc.vector.tensor_tensor(steps_tmp[:, 5, 0:NJ], steps_tmp[:, 1, 0:NJ], steps_tmp[:, 4, 0:NJ],
                                                ALU.subtract))
                    run(nc.vector.tensor_copy(steps_int[:, 1, :], steps_tmp[:, 4, 0:NJ]))
                    run(nc.vector.tensor_copy(steps_int[:, 2, :], steps_tmp[:, 5, 0:NJ]))
                    run(nc.vector.tensor_scalar(steps_tmp[:, 6, 0:NJ], steps_tmp[:, 5, 0:NJ], float(P), None, ALU.mult))
                    n.vec = run.count

                @block.gpsimd
                def _(pool):
                    pool.wait_ge(s.vec, n.vec)
                    for j in range(NJ):
                        for to, of in ((src_i, src), (dst_i, dst), (scratch[:, 2 * S:3 * S], ew)):
                            pool.indirect_dma_start(
                                out=to[:, j * P:(j + 1) * P], out_offset=None, in_=of[:, :],
                                in_offset=bass.IndirectOffsetOnAxis(ap=steps_int[:, 1, j:j + 1].bitcast(U32), axis=0),
                            ).then_inc(s.tiles_in, 16)
                    pool.wait_ge(s.tiles_in, 3 * NJ * 16)

                @block.sync
                def _(sp):
                    sp.wait_ge(s.vec, n.vec)
                    sp.dma_start(d.tile_of.rearrange("(j p) -> p j", p=P), steps_int[:, 1, :], allow_slow_non_contiguous=True).then_inc(s.stored, 16)
                    sp.dma_start(d.block_of.rearrange("(j p) -> p j", p=P), steps_int[:, 2, :], allow_slow_non_contiguous=True).then_inc(s.stored, 16)
                    n.stored += 32
                    sp.wait_ge(s.stored, n.stored)
            with nc.Block() as block:
                tables = ((0, src_col), (1, lane_col), (2, w_col))
                batches = [(j, min(4, NJ - j)) for j in range(0, NJ, 4)]
                start_v = n.vec

                @block.vector
                def _(dve):
                    run = chain(dve, "vec")
                    run(nc.vector.tensor_copy(scratch[:, 0:S], src_i))
                    for j in range(NJ):
                        cut = scratch[:, S + j * P:S + (j + 1) * P]
                        run(nc.vector.tensor_scalar(cut, cut.bitcast(I32), steps_tmp[:, 6, j:j + 1], None,
                                                    ALU.subtract))
                    run(nc.vector.memset(edge_val[:, 0, :], -BIG))
                    made = 0
                    for t, to in tables:
                        for j, m in batches:
                            made += 1
                            dve.wait_ge(s.batch_t, n.batch + made)
                            half = pa[:, (made % 2) * 512:(made % 2) * 512 + m * P]
                            nc.vector.tensor_copy(to[:, j * P:(j + m) * P], half).then_inc(s.batch_copied, 1)
                    dve.wait_ge(s.batch_copied, n.batch + made)
                    run(nc.vector.tensor_copy(src_col[:, S:S + BODY], src_col[:, 0:BODY]))
                    run(nc.vector.tensor_copy(lane_col[:, S:S + BODY], lane_col[:, 0:BODY]))
                    run(nc.vector.memset(acc[:, :, :], 0.0))
                    n.vec = run.count

                @block.tensor
                def _(pe):
                    pe.wait_ge(s.vec, start_v + 1 + NJ)
                    made = 0
                    for t, _to in tables:
                        for j, m in batches:
                            made += 1
                            if made > 2:
                                pe.wait_ge(s.batch_copied, n.batch + made - 2)
                            for q in range(m):
                                last = nc.tensor.transpose(pa[:, (made % 2) * 512 + q * P:(made % 2) * 512 + (q + 1) * P],
                                                           scratch[:, t * S + (j + q) * P:t * S + (j + q + 1) * P],
                                                           ident[:, :])
                            last.then_inc(s.batch_t, 1)

                @block.sync
                def _(sp):
                    load(sp, walk_sb[0:1, :], d.block_of.unsqueeze(0))
                    load(sp, walk_sb[32:33, :], d.tile_of.unsqueeze(0))
                    sp.wait_ge(s.vec, start_v + 2 + NJ)
                    rows_of = scratch[:, 0:2 * S].rearrange("p (t j e) -> p t j e", t=2, e=P)
                    load(sp, d.src_rows.rearrange("(j p) e -> p j e", p=P), rows_of[:, 0])
                    load(sp, lane_rows.rearrange("(j p) e -> p j e", p=P), rows_of[:, 1])
                    load(sp, d.lane[0:1].unsqueeze(0), edge_val[0:1, 0, :])
                    load(sp, d.lane[S * P + 1:S * P + 2].unsqueeze(0), edge_val[0:1, 0, :])
                    sp.wait_ge(s.loaded, n.loaded)
            n.batch += 3 * len(batches)

        CH = max(c for c in range(1, 8) if NB % c == 0)
        feats = xcur[:, :, 0:F]
        spare = acc[:, :, FX:FX + F]
        last_lanes = N - (NB - 1) * P

        def layer_norm():
            with nc.Block() as block:
                @block.vector
                def _(dve):
                    run = chain(dve, "vec")
                    run(nc.vector.tensor_reduce(col[:, 0, :], feats, AX.X, ALU.add))
                    run(nc.vector.tensor_scalar(col[:, 0, :], col[:, 0, :], 1.0 / F, None, ALU.mult))
                    run(nc.vector.tensor_tensor(feats, feats, all_lanes(col[:, 0, :], F), ALU.subtract))
                    run(nc.vector.tensor_tensor(spare, feats, feats, ALU.mult))
                    run(nc.vector.tensor_reduce(col[:, 1, :], spare, AX.X, ALU.add))
                    run(nc.vector.tensor_scalar(col[:, 1, :], col[:, 1, :], 1.0 / F, 1e-5, ALU.mult, ALU.add))
                    dve.wait_ge(s.act, n.act + 1)
                    run(nc.vector.reciprocal(col[:, 3, :], col[:, 2, :]))
                    run(nc.vector.tensor_tensor(feats, feats, all_lanes(col[:, 3, :], F), ALU.mult))
                    n.vec = run.count

                @block.scalar
                def _(act):
                    act.wait_ge(s.vec, n.vec - 2)
                    nc.scalar.activation(col[:, 2, :], col[:, 1, :], ACT.Sqrt).then_inc(s.act, 1)
                    n.act += 1

        def project(view, depth, weights, width, kind):
            base = n.proj
            rounds = NB // CH
            n.proj += rounds
            heads = len(view.shape) == 4
            with nc.Block() as block:
                @block.gpsimd
                def _(pool):
                    with pool.Fori(0, rounds) as i:
                        pool.wait_ge(s.proj_t, i + (base + 1))
                        if heads:
                            to = proj_in[:, 0:CH * depth].rearrange("p (b h f) -> p b h f", b=CH, h=2)
                        else:
                            to = proj_in[:, 0:CH * depth].rearrange("p (b f) -> p b f", b=CH)
                        if heads:
                            for h in range(2):
                                last = nc.gpsimd.tensor_copy(to[:, :, h, :], view[:, bass.ds(i * CH, CH), h, :])
                        else:
                            last = nc.gpsimd.tensor_copy(to, view[:, bass.ds(i * CH, CH), :])
                        last.then_inc(s.proj_in, 1)

                @block.tensor
                def _(pe):
                    with pe.Fori(0, rounds) as i:
                        pe.wait_ge(s.proj_in, i + (base + 1))
                        for c in range(CH):
                            last = nc.tensor.matmul(pa[0:depth, c * P:(c + 1) * P],
                                                    proj_in[:, c * depth:(c + 1) * depth], ident[:, :],
                                                    start=True, stop=True)
                        last.then_inc(s.proj_t, 1)
                        pe.wait_ge(s.proj_copied, i + (base + 1))
                        pe.wait_ge(s.proj_out, i + (base + 1))
                        for c in range(CH):
                            last = nc.tensor.matmul(pb[:, c * width:(c + 1) * width],
                                                    proj_tr[0:depth, c * P:(c + 1) * P], weights,
                                                    start=True, stop=True)
                        last.then_inc(s.proj_mm, 1)

                @block.scalar
                def _(act):
                    with act.Fori(0, rounds) as i:
                        act.wait_ge(s.proj_t, i + (base + 2))
                        nc.scalar.copy(proj_tr[0:depth, 0:CH * P], pa[0:depth, 0:CH * P]).then_inc(s.proj_copied, 1)

                @block.vector
                def _(dve):
                    with dve.Fori(0, rounds) as i:
                        got = pb[:, 0:CH * width].rearrange("p (b f) -> p b f", b=CH)
                        dve.wait_ge(s.proj_mm, i + (base + 1))
                        if kind == "hop1":
                            by = dinv[:, bass.ds(i * CH, CH)].unsqueeze(2).to_broadcast([P, CH, width])
                            nc.vector.tensor_tensor(acc[:, bass.ds(i * CH, CH), 0:width], got, by,
                                                    ALU.mult).then_inc(s.proj_out, 1)
                        if kind == "gcn":
                            to = xcur[:, bass.ds(i * CH, CH), 0:F]
                            nc.vector.tensor_tensor(to, to, got, ALU.add).then_inc(s.proj_out, 1)
                        if kind == "heads":
                            nc.vector.tensor_copy(acc[:, bass.ds(i * CH, CH), 0:F], got).then_inc(s.proj_out, 1)

        def fill_idx(act, table, at, half):
            act.activation(idx[:, half * RING:(half + 1) * RING], table[:, at], ACT.Copy).then_inc(s.idx_filled, 1)

        def block_numbers(engine, i, k):
            return nc.values_load_multi_w_load_instructions(
                walk_sb[0:1, bass.ds(i * BODY + k, RING)], engines=[engine], min_val=0, max_val=NB - 1,
                skip_runtime_bounds_check_because="steps less tiles, which lies within the blocks")[1]

        def gathers(block, walk_no, table, width, freed, freed_base):
            @block.gpsimd
            def _(pool):
                filled, free = pool.alloc_register(f"filled{walk_no}"), pool.alloc_register(f"free{walk_no}")
                pool.reg_mov(filled, 2 * walk_no * ITS + 1)
                pool.reg_mov(free, freed_base + GROUP)
                with pool.Fori(0, ITS) as _i:
                    for k in range(BODY):
                        if k % RING == 0:
                            pool.wait_ge(s.idx_filled, filled)
                            pool.reg_add(filled, filled, 1)
                        if k % GROUP == 0:
                            pool.wait_ge(freed, free)
                            pool.reg_add(free, free, GROUP)
                        pool.indirect_dma_start(
                            out=rows[:, k % RING, 0:width], out_offset=None, in_=table,
                            in_offset=bass.IndirectOffsetOnAxis(ap=idx[:, k:k + 1], axis=0),
                        ).then_inc(s.gathered[k % RING // GROUP], 16)

        def gathered_by(walk_no, i, k):
            return i * (2 * 16 * GROUP) + (walk_no * S * 4 + 16 * GROUP * (k // RING + 1))

        def sum_by_lane(kind, agg_no, width, table=None, walk_no=None):
            base = agg_no * S
            with nc.Block() as block:
                if table is not None:
                    gathers(block, walk_no, table, width if kind != "weighted" else F, s.matmuls, base)

                @block.scalar
                def _(act):
                    if kind == "heads":
                        act.sem_inc(s.scaled, RING)
                    if walk_no == 0:
                        for half in range(2):
                            fill_idx(act, src_col, slice(half * RING, (half + 1) * RING), half)
                    with act.Fori(0, ITS) as i:
                        for k in range(0, BODY, GROUP):
                            q = k % RING // GROUP
                            if kind == "weighted":
                                act.wait_ge(s.gathered[q], gathered_by(walk_no, i, k))
                                for j in range(k, k + GROUP):
                                    nc.scalar.activation(side[:, j % RING, 0:F], rows[:, j % RING, 0:F], ACT.Copy,
                                                         scale=w_col[:, bass.ds(i * BODY + j, 1)],
                                                         ).then_inc(s.weighted, 1)
                            if kind == "heads":
                                half = k // (2 * GROUP) % 2
                                if k % (2 * GROUP) == 0:
                                    act.wait_ge(s.reloaded[half], i * 32 + (16 + 16 * (k // RING)))
                                act.wait_ge(s.matmuls, i * BODY + (RING + base + k + GROUP - 2 * GROUP))
                                for j in range(k, k + GROUP):
                                    for h in range(2):
                                        last = nc.scalar.activation(
                                            pair[:, j % (2 * GROUP), h * FX:(h + 1) * FX],
                                            rows[:, half * 2 * GROUP + j % (2 * GROUP), :], ACT.Copy,
                                            scale=scratch[:, bass.ds(i * BODY + (h * S + j), 1)])
                                    last.then_inc(s.scaled, 1)
                            if table is not None and q == RING // GROUP - 1:
                                half = k // RING
                                act.wait_ge(s.matmuls, i * BODY + (RING + base + half * RING + RING))
                                fill_idx(act, src_col, bass.ds(i * BODY + (BODY + half * RING), RING)
                                         , half)

                @block.vector
                def _(dve):
                    def make_onehots(at, slot):
                        nc.vector.tensor_tensor(
                            onehot[:, slot * GROUP:(slot + 1) * GROUP, :],
                            lanes_free[:, :].unsqueeze(1).to_broadcast([P, GROUP, P]),
                            lane_col[:, at].unsqueeze(2).to_broadcast([P, GROUP, P]),
                            ALU.is_equal).then_inc(s.onehots, 1)

                    if agg_no == 0:
                        dve.sem_inc(s.adds, SUMS)
                        make_onehots(slice(0, GROUP), 0)
                    if kind == "plain_dups":
                        dve.sem_inc(s.dup_counted, RING)
                    with dve.Fori(0, ITS) as i:
                        for k in range(0, BODY, GROUP):
                            if k % RING == 0:
                                blocks_of = block_numbers(mybir.EngineType.DVE, i, k)
                            dve.wait_ge(s.matmuls, i * BODY + (RING + base + k))
                            make_onehots(bass.ds(i * BODY + (k + GROUP), GROUP), (k // GROUP + 1) % 2)
                            slot = k // GROUP % 2
                            if kind == "plain_hist":
                                dve.wait_ge(s.hist_used, i * (BODY // GROUP) + (k // GROUP + 1))
                                lo = hist_lo[:, slot * GROUP:(slot + 1) * GROUP, :]
                                hi = hist_hi[:, slot * GROUP:(slot + 1) * GROUP, :]
                                at = i * BODY + k
                                nc.vector.tensor_tensor(
                                    lo, lanes_free[:, :].unsqueeze(1).to_broadcast([P, GROUP, P]),
                                    scratch[:, bass.ds(at, GROUP)].unsqueeze(2).to_broadcast([P, GROUP, P]),
                                    ALU.is_equal).then_inc(s.hist_ready, 1)
                                nc.vector.tensor_tensor(
                                    hi, lanes_free[:, 0:NB].unsqueeze(1).to_broadcast([P, GROUP, NB]),
                                    scratch[:, bass.ds(at + S, GROUP)].unsqueeze(2).to_broadcast([P, GROUP, NB]),
                                    ALU.is_equal).then_inc(s.hist_ready, 1)
                            dve.wait_ge(s.matmuls, i * BODY + (RING + base + k + GROUP))
                            for j in range(k, k + GROUP):
                                dve.wait_ge(s.adds, i * BODY + (SUMS + base + j))
                                to = acc[:, bass.ds(blocks_of[j % RING], 1), 0:width].rearrange("p o f -> p (o f)")
                                nc.vector.tensor_tensor(to, to, sums[:, j % SUMS, 0:width],
                                                        ALU.add).then_inc(s.adds, 1)
                                if kind == "plain_dups":
                                    half = k // (2 * GROUP) % 2
                                    if j % (2 * GROUP) == 0:
                                        dve.wait_ge(s.src_loaded[half], i * 32 + 16 * (k // RING + 1))
                                    m = j % (2 * GROUP)
                                    nc.vector.scalar_tensor_tensor(
                                        one_dup[:, :], bcast[:, half, m * P:(m + 1) * P],
                                        src_col[:, bass.ds(i * BODY + j, 1)], earlier[:, :],
                                        ALU.is_equal, ALU.mult,
                                        accum_out=scratch[:, bass.ds(i * BODY + j, 1)]).then_inc(s.dup_counted, 1)
                                    dve.wait_ge(s.dup_counted, i * BODY + (RING + j + 1))
                            if kind == "plain_hist":
                                dve.wait_ge(s.hist_ready, i * (3 * BODY // GROUP) + (3 * (k // GROUP) + 2))
                                nc.vector.tensor_tensor(
                                    hi, hi, scratch[:, bass.ds(at + 2 * S, GROUP)].unsqueeze(2)
                                    .to_broadcast([P, GROUP, NB]), ALU.mult).then_inc(s.hist_ready, 1)

                @block.tensor
                def _(pe):
                    if agg_no == 0:
                        pe.sem_inc(s.matmuls, RING)
                    if kind == "plain_hist":
                        pe.sem_inc(s.hist_used, 2)
                        nc.tensor.matmul(hist[:, 0:NB], zeros[:, 0:P], zeros[:, 0:NB], start=True, stop=False)
                    with pe.Fori(0, ITS) as i:
                        for k in range(0, BODY, GROUP):
                            q = k % RING // GROUP
                            if kind == "weighted":
                                pe.wait_ge(s.weighted, i * BODY + (k + GROUP))
                            elif kind == "heads":
                                pe.wait_ge(s.scaled, i * BODY + (RING + k + GROUP))
                            else:
                                pe.wait_ge(s.gathered[q], gathered_by(walk_no, i, k))
                            pe.wait_ge(s.onehots, i * (BODY // GROUP) + (base // GROUP + k // GROUP + 1))
                            pe.wait_ge(s.adds, i * BODY + (SUMS + base + k + GROUP - SUMS))
                            for j in range(k, k + GROUP):
                                if kind == "weighted":
                                    of = side[:, j % RING, :]
                                elif kind == "heads":
                                    of = pair[:, j % (2 * GROUP), :]
                                else:
                                    of = rows[:, j % RING, 0:width]
                                nc.tensor.matmul(sums[:, j % SUMS, 0:width], onehot[:, j % (2 * GROUP), :], of,
                                                 start=True, stop=True).then_inc(s.matmuls, 1)
                            if kind == "plain_hist":
                                pe.wait_ge(s.hist_ready, i * (3 * BODY // GROUP) + (3 * (k // GROUP) + 3))
                                slot = k // GROUP % 2
                                for j in range(slot * GROUP, (slot + 1) * GROUP):
                                    last = nc.tensor.matmul(hist[:, 0:NB], hist_lo[:, j, :], hist_hi[:, j, :],
                                                            start=False, stop=False)
                                last.then_inc(s.hist_used, 1)
                    if kind == "plain_hist":
                        pe.wait_ge(s.hist_used, 2 + S // GROUP)
                        nc.tensor.matmul(hist[:, 0:NB], zeros[:, 0:P], zeros[:, 0:NB], start=False,
                                         stop=True).then_inc(s.hist_used, 1)

                @block.sync
                def _(sp):
                    if kind == "plain_dups":
                        free = sp.alloc_register("src_halves")
                        sp.reg_mov(free, 2 * GROUP)
                        with sp.Fori(0, ITS) as i:
                            for c in range(BODY // (2 * GROUP)):
                                sp.wait_ge(s.dup_counted, free)
                                sp.reg_add(free, free, 2 * GROUP)
                                of = d.src_rows[bass.ds(i * BODY + c * 2 * GROUP, 2 * GROUP), :]
                                sp.dma_start(bcast[:, c % 2, :], of.rearrange("s e -> (s e)").partition_broadcast(P),
                                             ).then_inc(s.src_loaded[c % 2], 16)
                    if kind == "heads":
                        free = sp.alloc_register("sum_halves")
                        sp.reg_mov(free, 2 * GROUP)
                        with sp.Fori(0, ITS) as i:
                            for c in range(BODY // (2 * GROUP)):
                                sp.wait_ge(s.scaled, free)
                                sp.reg_add(free, free, 2 * GROUP)
                                at = i * (BODY * FX) + c * 2 * GROUP * FX
                                half = c % 2
                                sp.dma_start(rows[:, half * 2 * GROUP:(half + 1) * 2 * GROUP, :]
                                             .rearrange("p s f -> p (s f)"),
                                             d.summed_edges[:, bass.ds(at, 2 * GROUP * FX)],
                                             ).then_inc(s.reloaded[half], 16)

        CHUNKS = BODY // CHUNK

        def chunk_in(sp, of, to, landed, at):
            sp.dma_start(to, of[bass.ds(at, CHUNK), :].rearrange("s e -> (s e)").partition_broadcast(P)
                         ).then_inc(landed, 16)

        def score_walk():
            walk_no = 3
            with nc.Block() as block:
                gathers(block, walk_no, d.nodes2, FX, s.scored, 0)

                @block.vector
                def _(dve):
                    dve.sem_inc(s.scored, RING)
                    dve.sem_inc(s.lane_onehots, 4)
                    with dve.Fori(0, ITS) as i:
                        for k in range(0, BODY, GROUP):
                            q, g = k % RING // GROUP, k // GROUP
                            half, slot = g // 2 % 2, g % 2
                            ops = i * (4 * BODY // GROUP) + 4 * g
                            if slot == 0:
                                dve.wait_ge(s.lane_loaded[half], i * 32 + 16 * (k // RING + 1))
                            dve.wait_ge(s.er_ready, i * (BODY // GROUP) + (g + 1))
                            nc.vector.tensor_scalar(
                                onehot2[:, slot * GROUP:(slot + 1) * GROUP, :].rearrange("p s e -> p (s e)"),
                                bcast2[:, half, slot * GROUP * P:(slot + 1) * GROUP * P], lane_id[:, 0:1], None,
                                ALU.is_equal).then_inc(s.lane_onehots, 1)
                            places = slice(k % RING, k % RING + GROUP)
                            u = side[:, places, 0:F]
                            dve.wait_ge(s.gathered[q], gathered_by(walk_no, i, k))
                            dve.wait_ge(s.bond_loaded[q], i * (2 * 16 * GROUP) + 16 * GROUP * (k // RING + 1))
                            nc.vector.tensor_tensor(u, u, rows[:, places, 0:F], ALU.add).then_inc(s.edge_sums, 1)
                            at = bass.ds(i * BODY + k, GROUP)
                            nc.vector.tensor_tensor(w_col[:, at], w_col[:, at],
                                                    rows[:, places, F:FX].rearrange("p s o -> p (s o)"),
                                                    ALU.mult).then_inc(s.edge_sums, 1)
                            dve.wait_ge(s.edge_sums, ops + 1)
                            nc.vector.tensor_tensor(
                                dots[:, :, :, :], u.unsqueeze(2).to_broadcast([P, GROUP, 2, F]),
                                v_rows[:, 0:2, :].unsqueeze(1).to_broadcast([P, GROUP, 2, F]),
                                ALU.mult).then_inc(s.edge_sums, 1)
                            dve.wait_ge(s.edge_sums, ops + 3)
                            nc.vector.tensor_reduce(dot_sums[:, :, :], dots[:, :, :, :], AX.X,
                                                    ALU.add).then_inc(s.edge_sums, 1)
                            dve.wait_ge(s.edge_sums, ops + 4)
                            dve.wait_ge(s.er_ready, i * (BODY // GROUP) + (g + 3))
                            nc.vector.tensor_tensor(
                                scratch[:, bass.ds(i * (2 * BODY) + 2 * k, 2 * GROUP)],
                                dot_sums[:, :, :].rearrange("p s h -> p (s h)"),
                                pa[:, slot * 512:slot * 512 + 2 * GROUP], ALU.add).then_inc(s.scored, GROUP)

                @block.tensor
                def _(pe):
                    pe.sem_inc(s.er_ready, 2)
                    with pe.Fori(0, ITS) as i:
                        for k in range(0, BODY, GROUP):
                            g, slot = k // GROUP, k // GROUP % 2
                            if k % RING == 0:
                                blocks_of = block_numbers(mybir.EngineType.PE, i, k)
                            pe.wait_ge(s.lane_onehots, i * (BODY // GROUP) + (4 + g + 1))
                            pe.wait_ge(s.scored, i * BODY + (k + 3 * GROUP))
                            for j in range(GROUP):
                                at = slot * 512 + 2 * j
                                last = nc.tensor.matmul(
                                    pa[:, at:at + 2], onehot2[:, slot * GROUP + j, :],
                                    er[:, bass.ds(blocks_of[(k + j) % RING], 1), :].rearrange("p o h -> p (o h)"),
                                    start=True, stop=True)
                            last.then_inc(s.er_ready, 1)

                @block.sync
                def _(sp):
                    lanes_free_at, places_free_at = sp.alloc_register("lanes_at"), sp.alloc_register("places_at")
                    sp.reg_mov(lanes_free_at, 2)
                    sp.reg_mov(places_free_at, 16)
                    with sp.Fori(0, ITS) as i:
                        for c in range(CHUNKS):
                            if c % 2 == 0:
                                tiles_of = nc.values_load_multi_w_load_instructions(
                                    walk_sb[32:33, bass.ds(i * BODY + c * CHUNK, RING)],
                                    engines=[mybir.EngineType.SP], min_val=0, max_val=T - 1,
                                    skip_runtime_bounds_check_because="a count of tiles, which lies within them")[1]
                            sp.wait_ge(s.lane_onehots, lanes_free_at)
                            sp.reg_add(lanes_free_at, lanes_free_at, 2)
                            chunk_in(sp, lane_rows, bcast2[:, c % 2, :], s.lane_loaded[c % 2], i * BODY + c * CHUNK)
                            sp.wait_ge(s.spilled[c % 2], places_free_at)
                            if c % 2 == 1:
                                sp.reg_add(places_free_at, places_free_at, 16)
                            for j in range(c * CHUNK, (c + 1) * CHUNK):
                                sp.dma_start(side[:, j % RING, 0:F],
                                             edge_attr[bass.ds(tiles_of[j % RING] * P, P), :],
                                             ).then_inc(s.bond_loaded[j % RING // GROUP], 16)

                @block.scalar
                def _(act):
                    for half in range(2):
                        act.sem_inc(s.spilled[half], 16)
                    with act.Fori(0, ITS) as i:
                        for c in range(CHUNKS):
                            half = c % 2
                            act.wait_ge(s.scored, i * BODY + (RING + (c + 1) * CHUNK))
                            act.dma_start(d.summed_edges[:, bass.ds(i * (BODY * FX) + c * CHUNK * FX, CHUNK * FX)],
                                          side[:, half * CHUNK:(half + 1) * CHUNK, :].rearrange("p s f -> p (s f)"),
                                          ).then_inc(s.spilled[half], 16)
                            if half == 1:
                                fill_idx(act, src_col, bass.ds(i * BODY + (BODY + (c // 2) * RING), RING), c // 2)
                    for half in range(2):
                        act.wait_ge(s.spilled[half], 16 + S // CHUNK // 2 * 16)

        batches4 = [(j, min(4, NJ - j)) for j in range(0, NJ, 4)]

        def transposed(block, sources, targets):
            base = n.batch
            n.batch += len(sources) * len(batches4)

            def on_pe(pe):
                made = base
                for source in sources:
                    for j, m in batches4:
                        made += 1
                        if made > base + 2:
                            pe.wait_ge(s.batch_copied, made - 2)
                        for q in range(m):
                            last = nc.tensor.transpose(pa[:, (made % 2) * 512 + q * P:(made % 2) * 512 + (q + 1) * P],
                                                       source(j + q), ident[:, :])
                        last.then_inc(s.batch_t, 1)

            def on_dve(dve):
                made = base
                for to in targets:
                    for j, m in batches4:
                        made += 1
                        dve.wait_ge(s.batch_t, made)
                        nc.vector.tensor_copy(to[:, j * P:(j + m) * P],
                                              pa[:, (made % 2) * 512:(made % 2) * 512 + m * P],
                                              ).then_inc(s.batch_copied, 1)
                dve.wait_ge(s.batch_copied, made)
            return on_pe, on_dve

        def edge_softmax():
            raw = scratch[:, 0:2 * S].rearrange("p (s h) -> p s h", h=2)
            by_row = [acc_flat[:, h * S:(h + 1) * S] for h in range(2)]
            score = [scratch[:, h * S:(h + 1) * S] for h in range(2)]
            lanes_x = acc_flat[:, 0:S + 2]
            new_seg = acc_flat[:, S + 2:2 * S + 3]
            fwd = acc_flat[:, 2 * S + 3:3 * S + 3]
            bwd = scratch[:, 2 * S:3 * S]

            with nc.Block() as block:
                on_pe, on_dve = transposed(block, [lambda j, h=h: raw[:, j * P:(j + 1) * P, h] for h in range(2)],
                                           by_row)

                @block.vector
                def _(dve):
                    run = chain(dve, "vec")
                    run(nc.vector.scalar_tensor_tensor(scratch[:, 0:2 * S], scratch[:, 0:2 * S], 0.2,
                                                       scratch[:, 0:2 * S], ALU.mult, ALU.max))
                    n.vec = run.count
                    on_dve(dve)
                    run(nc.vector.memset(carry_in[:, :, :], -BIG))
                    n.vec = run.count

                @block.tensor
                def _(pe):
                    pe.wait_ge(s.vec, n.vec - 1)
                    on_pe(pe)

                @block.gpsimd
                def _(pool):
                    nc.gpsimd.memset(clear, 0.0).then_inc(s.pool, 1)
                    n.pool += 1
                    pool.wait_ge(s.pool, n.pool)
                    for t in range(TABLES):
                        cuts = d.scattered[t].rearrange("(c p b) f -> c p (b f)", c=TABLE_CUTS, p=P)
                        for c in range(TABLE_CUTS):
                            pool.dma_start(cuts[c], clear).then_inc(s.scatter_done[t], 16)
                    for t in range(TABLES):
                        pool.wait_ge(s.scatter_done[t], 16 * TABLE_CUTS)

                @block.sync
                def _(sp):
                    sp.wait_ge(s.batch_copied, n.batch)
                    for h in range(2):
                        sp.dma_start(d.scores[h].rearrange("(j p) e -> p j e", p=P),
                                     by_row[h].rearrange("p (j e) -> p j e", e=P)).then_inc(s.stored, 16)
                    n.stored += 32
                    sp.wait_ge(s.stored, n.stored)
                    for h in range(2):
                        load(sp, score[h], d.scores[h].rearrange("(p j) e -> p (j e)", p=P))
                    load(sp, lanes_x, bass.AP(d.lane.tensor, 0, [[S, P], [1, S + 2]]))
                    sp.wait_ge(s.loaded, n.loaded)

            def scans(run, h, first_f, first_b):
                run(nc.vector.tensor_tensor_scan(fwd, new_seg[:, 0:S], score[h], first_f, ALU.add, ALU.max))
                run(nc.vector.tensor_tensor_scan(bwd[:, ::-1], new_seg[:, S:0:-1], score[h][:, ::-1],
                                                 first_b, ALU.add, ALU.max))

            with nc.Block() as block:
                @block.vector
                def _(dve):
                    run = chain(dve, "vec")
                    run(nc.vector.tensor_tensor(new_seg, lanes_x[:, 0:S + 1], lanes_x[:, 1:S + 2], ALU.not_equal))
                    run(nc.vector.tensor_scalar(new_seg, new_seg, -BIG, None, ALU.mult))
                    run(nc.vector.tensor_reduce(edge_val[:, 4, :], new_seg[:, 0:S], AX.X, ALU.min))
                    run(nc.vector.tensor_reduce(edge_val[:, 5, :], new_seg[:, 1:S + 1], AX.X, ALU.min))
                    for h in range(2):
                        scans(run, h, -BIG, -BIG)
                        run(nc.vector.tensor_copy(edge_val[:, 2 * h, :], fwd[:, S - 1:S]))
                        run(nc.vector.tensor_copy(edge_val[:, 2 * h + 1, :], bwd[:, 0:1]))
                    n.vec = run.count

                @block.tensor
                def _(pe):
                    run = chain(pe, "pe")
                    pe.wait_ge(s.vec, n.vec)
                    for c in range(6):
                        run(nc.tensor.matmul(pa[0:1, c * P:(c + 1) * P], edge_val[:, c, :], ident[:, :],
                                             start=True, stop=True))
                    n.pe = run.count
            with nc.Block() as block:
                @block.vector
                def _(dve):
                    run = chain(dve, "vec")
                    run(nc.vector.tensor_copy(carry[:, :, :].rearrange("o c p -> o (c p)"), pa[0:1, 0:6 * P]))
                    for h in range(2):
                        run(nc.vector.tensor_tensor_scan(carry_in[:, 2 * h, 1:P + 1], carry[:, 4, :],
                                                         carry[:, 2 * h, :], -BIG, ALU.add, ALU.max))
                        run(nc.vector.tensor_tensor_scan(carry_in[:, 2 * h + 1, P - 1::-1], carry[:, 5, ::-1],
                                                         carry[:, 2 * h + 1, ::-1], -BIG, ALU.add, ALU.max))
                    n.vec = run.count

                @block.tensor
                def _(pe):
                    run = chain(pe, "pe")
                    pe.wait_ge(s.vec, n.vec)
                    for c in range(4):
                        run(nc.tensor.matmul(pb[:, c:c + 1], carry_in[:, c, c % 2:c % 2 + P], ones[0:1, 0:1],
                                             start=True, stop=True))
                    n.pe = run.count
            with nc.Block() as block:
                @block.vector
                def _(dve):
                    run = chain(dve, "vec")
                    run(nc.vector.tensor_copy(carry_out[:, :], pb[:, 0:4]))
                    for h in range(2):
                        scans(run, h, carry_out[:, 2 * h:2 * h + 1], carry_out[:, 2 * h + 1:2 * h + 2])
                        run(nc.vector.tensor_tensor(fwd, fwd, bwd, ALU.max))
                        run(nc.vector.tensor_tensor(score[h], score[h], fwd, ALU.subtract))
                    n.vec = run.count

                @block.scalar
                def _(act):
                    run = chain(act, "act")
                    for h in range(2):
                        act.wait_ge(s.vec, n.vec - (4 if h == 0 else 0))
                        run(nc.scalar.activation(score[h], score[h], ACT.Exp))
                    n.act = run.count

                @block.sync
                def _(sp):
                    for h in range(2):
                        sp.wait_ge(s.act, n.act - 1 + h)
                        sp.dma_start(d.weights[h].rearrange("(p j) e -> p (j e)", p=P), score[h]
                                     ).then_inc(s.stored, 16)
                    n.stored += 32
                    sp.wait_ge(s.stored, n.stored)
                    for h in range(2):
                        load(sp, by_row[h].rearrange("p (j e) -> p j e", e=P),
                             d.weights[h].rearrange("(j p) e -> p j e", p=P))
                    sp.wait_ge(s.loaded, n.loaded)
            with nc.Block() as block:
                on_pe, on_dve = transposed(
                    block, [lambda j, h=h: acc_flat[:, h * S + j * P:h * S + (j + 1) * P] for h in range(2)],
                    [scratch[:, h * S:(h + 1) * S] for h in range(2)])

                @block.vector
                def _(dve):
                    run = chain(dve, "vec")
                    on_dve(dve)
                    run(nc.vector.memset(acc[:, :, :], 0.0))
                    n.vec = run.count

                @block.tensor
                def _(pe):
                    on_pe(pe)

        def scatter_walk():
            with nc.Block() as block:
                @block.gpsimd
                def _(pool):
                    filled, ready = pool.alloc_register("filled4"), pool.alloc_register("ready")
                    pool.reg_mov(filled, n.idx + 1)
                    pool.reg_mov(ready, 2 + 1)
                    over = [pool.alloc_register(f"over{t}") for t in range(TABLES)]
                    for t in range(TABLES):
                        pool.reg_mov(over[t], 16 * TABLE_CUTS)
                    with pool.Fori(0, ITS) as _i:
                        for k in range(BODY):
                            if k % RING == 0:
                                pool.wait_ge(s.idx_filled, filled)
                                pool.reg_add(filled, filled, 1)
                            if k % GROUP == 0:
                                pool.wait_ge(s.merged_out, ready)
                                pool.reg_add(ready, ready, 1)
                            t = k % TABLES
                            pool.wait_ge(s.scatter_done[t], over[t])
                            pool.reg_add(over[t], over[t], 16)
                            pool.indirect_dma_start(
                                out=d.scattered[t], out_offset=bass.IndirectOffsetOnAxis(ap=idx[:, k:k + 1], axis=0),
                                in_=rows[:, k % RING, :], in_offset=None, compute_op=ALU.add,
                            ).then_inc(s.scatter_done[t], 16)
                    for t in range(TABLES):
                        pool.wait_ge(s.scatter_done[t], 16 * TABLE_CUTS + 16 * (S // TABLES))

                @block.vector
                def _(dve):
                    dve.sem_inc(s.equal_ready, 4)
                    with dve.Fori(0, ITS) as i:
                        for k in range(0, BODY, GROUP):
                            g, half, slot = k // GROUP, k // CHUNK % 2, k // GROUP % 2
                            if slot == 0:
                                dve.wait_ge(s.lane_loaded[half], i * 32 + (32 * ITS + 16 * (k // RING + 1)))
                                dve.wait_ge(s.src_loaded[half], i * 32 + (32 * ITS + 16 * (k // RING + 1)))
                            dve.wait_ge(s.merged, i * (BODY // GROUP) + (g + 1))
                            nc.vector.tensor_scalar(
                                onehot2[:, slot * GROUP:(slot + 1) * GROUP, :].rearrange("p s e -> p (s e)"),
                                bcast2[:, half, slot * GROUP * P:(slot + 1) * GROUP * P], lane_id[:, 0:1], None,
                                ALU.is_equal).then_inc(s.lane_onehots, 1)
                            nc.vector.tensor_tensor(
                                onehot[:, slot * GROUP:(slot + 1) * GROUP, :],
                                bcast[:, half, slot * GROUP * P:(slot + 1) * GROUP * P]
                                .rearrange("p (s e) -> p s e", e=P),
                                src_col[:, bass.ds(i * BODY + k, GROUP)].unsqueeze(2).to_broadcast([P, GROUP, P]),
                                ALU.is_equal).then_inc(s.equal_ready, 1)

                @block.tensor
                def _(pe):
                    pe.sem_inc(s.merged, 2)
                    with pe.Fori(0, ITS) as i:
                        for k in range(0, BODY, GROUP):
                            g, slot = k // GROUP, k // GROUP % 2
                            if k % RING == 0:
                                blocks_of = block_numbers(mybir.EngineType.PE, i, k)
                            pe.wait_ge(s.equal_ready, i * (BODY // GROUP) + (4 + g + 1))
                            for j in range(GROUP):
                                nc.tensor.matmul(
                                    sums[:, slot * GROUP + j, 0:FX], onehot2[:, slot * GROUP + j, :],
                                    xcur[:, bass.ds(blocks_of[(k + j) % RING], 1), :].rearrange("p o f -> p (o f)"),
                                    start=True, stop=True).then_inc(s.spread, 1)
                            pe.wait_ge(s.values_ready, i * BODY + (k + GROUP))
                            pe.wait_ge(s.merged_out, i * (BODY // GROUP) + (g + 1))
                            for j in range(GROUP):
                                last = nc.tensor.matmul(pa[:, slot * 512 + j * FX:slot * 512 + (j + 1) * FX],
                                                        onehot[:, slot * GROUP + j, :],
                                                        side[:, slot * GROUP + j, :], start=True, stop=True)
                            last.then_inc(s.merged, 1)

                @block.scalar
                def _(act):
                    act.sem_inc(s.merged_out, 2)
                    fill_idx(act, scatter_col, slice(0, RING), 0)
                    with act.Fori(0, ITS) as i:
                        for k in range(0, BODY, GROUP):
                            g, slot = k // GROUP, k // GROUP % 2
                            act.wait_ge(s.merged, i * (BODY // GROUP) + (g + 1))
                            act.wait_ge(s.spread, i * BODY + (k + GROUP))
                            for j in range(GROUP):
                                nc.scalar.activation(side[:, slot * GROUP + j, :],
                                                     sums[:, slot * GROUP + j, 0:FX], ACT.Copy,
                                                     scale=scratch[:, bass.ds(i * BODY + (k + j), 1)],
                                                     ).then_inc(s.values_ready, 1)
                            act.wait_ge(s.merged, i * (BODY // GROUP) + (g + 3))
                            for j in range(k, k + GROUP):
                                act.wait_ge(s.scatter_done[j % TABLES],
                                            i * (16 * BODY // TABLES) + 16 * (TABLE_CUTS + j // TABLES - 1))
                            nc.scalar.copy(
                                rows[:, k % RING:k % RING + GROUP, :].rearrange("p s f -> p (s f)"),
                                pa[:, slot * 512:slot * 512 + GROUP * FX]).then_inc(s.merged_out, 1)
                            if k % RING == RING - GROUP:
                                if k < RING:
                                    fill_idx(act, scatter_col, bass.ds(i * BODY + RING, RING), 1)
                                else:
                                    fill_idx(act, scatter_col, bass.ds(i * BODY + BODY, RING), 0)

                @block.sync
                def _(sp):
                    free = sp.alloc_register("scatter_halves")
                    sp.reg_mov(free, 2)
                    with sp.Fori(0, ITS) as i:
                        for c in range(CHUNKS):
                            sp.wait_ge(s.equal_ready, free)
                            sp.reg_add(free, free, 2)
                            at = i * BODY + c * CHUNK
                            chunk_in(sp, lane_rows, bcast2[:, c % 2, :], s.lane_loaded[c % 2], at)
                            chunk_in(sp, d.src_rows, bcast[:, c % 2, :], s.src_loaded[c % 2], at)

        def after_weighted_sum():
            with nc.Block() as block:
                @block.vector
                def _(dve):
                    run = chain(dve, "vec")
                    run(nc.vector.tensor_tensor(feats, feats, acc[:, :, 0:F], ALU.add))
                    run(nc.vector.tensor_scalar(col[:, 4, :], acc[:, :, F], 1.0, None, ALU.add))
                    run(nc.vector.reciprocal(col[:, 5, :], col[:, 4, :]))
                    n.vec = run.count

                @block.scalar
                def _(act):
                    act.wait_ge(s.vec, n.vec)
                    nc.scalar.activation(dinv[:, :], col[:, 5, :], ACT.Sqrt).then_inc(s.act, 1)
                    n.act += 1

        def before_hop1():
            lo, hi, sq = (scratch[:, t * S:(t + 1) * S] for t in range(3))
            junk = acc_flat
            with nc.Block() as block:
                @block.vector
                def _(dve):
                    run = chain(dve, "vec")
                    run(nc.vector.tensor_scalar(hi, lane_col[:, 0:S], -0.5, None, ALU.is_gt))
                    run(nc.vector.tensor_scalar(lo, lane_col[:, 0:S], P - 0.5, None, ALU.is_lt))
                    run(nc.vector.tensor_tensor(lo, lo, hi, ALU.mult))
                    run(nc.vector.tensor_tensor(sq, w_col[:, :], w_col[:, :], ALU.mult))
                    run(nc.vector.tensor_tensor(sq, sq, lo, ALU.mult))
                    run(nc.vector.tensor_copy(lo.bitcast(I32), src_col[:, 0:S]))
                    run(nc.vector.tensor_scalar(hi.bitcast(I32), lo.bitcast(I32), 7, None, ALU.arith_shift_right))
                    run(nc.vector.tensor_copy(hi, hi.bitcast(I32)))
                    run(nc.vector.scalar_tensor_tensor(lo, hi, -float(P), src_col[:, 0:S], ALU.mult, ALU.add))
                    n.vec = run.count

                @block.sync
                def _(sp):
                    sp.dma_start(d.hop1.rearrange("(b p) f -> p b f", p=P), acc[:, :, 0:H]).then_inc(s.stored, 16)
                    n.stored += 16
                    sp.wait_ge(s.stored, n.stored)

        def between_hops():
            with nc.Block() as block:
                @block.vector
                def _(dve):
                    run = chain(dve, "vec")
                    by = all_lanes(dinv[:, :], H)
                    z = acc[:, :, 0:H]
                    run(nc.vector.tensor_tensor(z, z, by, ALU.mult))
                    run(nc.vector.tensor_tensor(z, z, b1_sb[:, :].unsqueeze(1).to_broadcast([P, NB, H]), ALU.add))
                    run(nc.vector.tensor_tensor(z, z, by, ALU.mult))
                    n.vec = run.count
                    dve.wait_ge(s.act, n.act + 1)
                    run(nc.vector.tensor_scalar(col[:, 5, :], col[:, 4, :], 1e-12, None, ALU.max))
                    run(nc.vector.reciprocal(inv_norm[:, :], col[:, 5, :]))
                    n.vec2 = run.count

                @block.scalar
                def _(act):
                    nc.scalar.activation(col[:, 4, :], hist[:, 0:NB], ACT.Sqrt).then_inc(s.act, 1)
                    n.act += 1

                @block.sync
                def _(sp):
                    sp.wait_ge(s.vec, n.vec)
                    sp.dma_start(d.hop2.rearrange("(b p) f -> p b f", p=P), acc[:, :, 0:H]).then_inc(s.stored, 16)
                    n.stored += 16
                    sp.wait_ge(s.stored, n.stored)
            n.vec = n.vec2

        def after_hops():
            with nc.Block() as block:
                @block.vector
                def _(dve):
                    run = chain(dve, "vec")
                    z = acc[:, :, 0:H]
                    run(nc.vector.tensor_tensor(z, z, all_lanes(dinv[:, :], H), ALU.mult))
                    run(nc.vector.tensor_tensor(feats, feats, b2_sb[:, :].unsqueeze(1).to_broadcast([P, NB, F]),
                                                ALU.add))
                    sc, tmp = scratch[:, 0:S], scratch[:, S:2 * S]
                    run(nc.vector.tensor_scalar(mask[:, :], lane_id[:, :], float(NB * P), None, ALU.add))
                    run(nc.vector.tensor_scalar(tmp, src_col[:, 0:S], mask[:, 0:1], None, ALU.subtract))
                    run(nc.vector.scalar_tensor_tensor(sc, sc, 0.0, tmp, ALU.is_equal, ALU.mult))
                    run(nc.vector.tensor_scalar(scatter_col[:, 0:S], sc, mask[:, 0:1], None, ALU.add))
                    run(nc.vector.tensor_copy(scatter_col[:, S:S + BODY], scatter_col[:, 0:BODY]))
                    n.vec = run.count

        def before_scores():
            with nc.Block() as block:
                @block.vector
                def _(dve):
                    run = chain(dve, "vec")
                    run(nc.vector.tensor_copy(xcur[:, :, F], inv_norm[:, :]))
                    n.vec = run.count
                    for h in range(2):
                        run(nc.vector.tensor_tensor(spare, feats,
                                                    v_rows[:, 2 + h, :].unsqueeze(1).to_broadcast([P, NB, F]),
                                                    ALU.mult))
                        run(nc.vector.tensor_reduce(er[:, :, h], spare, AX.X, ALU.add))
                    n.vec2 = run.count

                @block.sync
                def _(sp):
                    sp.wait_ge(s.vec, n.vec)
                    sp.dma_start(d.nodes2.rearrange("(b p) f -> p b f", p=P), xcur[:, :, :]).then_inc(s.stored, 16)
                    n.stored += 16
                    sp.wait_ge(s.stored, n.stored)
            n.vec = n.vec2

        heads4 = acc[:, :, :].rearrange("p b (h f) -> p b h f", h=2)

        def head_means():
            with nc.Block() as block:
                @block.vector
                def _(dve):
                    run = chain(dve, "vec")
                    for h in range(2):
                        run(nc.vector.tensor_scalar(col[:, h, :], heads4[:, :, h, F], 1e-30, None, ALU.max))
                        run(nc.vector.reciprocal(col[:, h, :], col[:, h, :]))
                        run(nc.vector.tensor_tensor(heads4[:, :, h, 0:F], heads4[:, :, h, 0:F],
                                                    all_lanes(col[:, h, :], F), ALU.mult))
                    n.vec = run.count

        def batch_norm():
            hv = acc[:, :, 0:F]
            last_block = acc[:, NB - 1, 0:F]

            def node_sum(view, to):
                with nc.Block() as block:
                    @block.vector
                    def _(dve):
                        run = chain(dve, "vec")
                        run(nc.vector.tensor_reduce(bn_sb[:, 2, :], view.rearrange("p b f -> p f b"), AX.X, ALU.add))
                        n.vec = run.count

                    @block.tensor
                    def _(pe):
                        run = chain(pe, "pe")
                        pe.wait_ge(s.vec, n.vec)
                        run(nc.tensor.matmul(pb[:, 0:F], ones[:, :], bn_sb[:, 2, :], start=True, stop=True))
                        n.pe = run.count
                with nc.Block() as block:
                    @block.vector
                    def _(dve):
                        run = chain(dve, "vec")
                        run(nc.vector.tensor_scalar(to, pb[:, 0:F], 1.0 / N, None, ALU.mult))
                        n.vec = run.count

            def all_nodes(ap):
                return ap.unsqueeze(1).to_broadcast([P, NB, F])

            with nc.Block() as block:
                @block.vector
                def _(dve):
                    run = chain(dve, "vec")
                    run(nc.vector.tensor_scalar(mask[:, :], lane_id[:, :], last_lanes - 0.5, None, ALU.is_lt))
                    run(nc.vector.tensor_scalar(last_block, last_block, mask[:, 0:1], None, ALU.mult))
                    n.vec = run.count
            node_sum(hv, bn_sb[:, 3, :])
            with nc.Block() as block:
                @block.vector
                def _(dve):
                    run = chain(dve, "vec")
                    run(nc.vector.tensor_tensor(hv, hv, all_nodes(bn_sb[:, 3, :]), ALU.subtract))
                    run(nc.vector.tensor_scalar(last_block, last_block, mask[:, 0:1], None, ALU.mult))
                    run(nc.vector.tensor_tensor(spare, hv, hv, ALU.mult))
                    n.vec = run.count
            node_sum(spare, bn_sb[:, 4, :])
            with nc.Block() as block:
                @block.vector
                def _(dve):
                    run = chain(dve, "vec")
                    run(nc.vector.tensor_scalar(bn_sb[:, 4, :], bn_sb[:, 4, :], 1e-5, None, ALU.add))
                    n.vec = run.count
                    dve.wait_ge(s.act, n.act + 1)
                    run(nc.vector.reciprocal(bn_sb[:, 4, :], bn_sb[:, 5, :]))
                    run(nc.vector.tensor_tensor(bn_sb[:, 4, :], bn_sb[:, 4, :], bn_sb[:, 0, :], ALU.mult))
                    run(nc.vector.tensor_tensor(hv, hv, all_nodes(bn_sb[:, 4, :]), ALU.mult))
                    run(nc.vector.tensor_tensor(hv, hv, all_nodes(bn_sb[:, 1, :]), ALU.add))
                    run(nc.vector.scalar_tensor_tensor(feats, hv, 0.0, feats, ALU.max, ALU.add))
                    n.vec2 = run.count

                @block.scalar
                def _(act):
                    act.wait_ge(s.vec, n.vec)
                    nc.scalar.activation(bn_sb[:, 5, :], bn_sb[:, 4, :], ACT.Sqrt).then_inc(s.act, 1)
                    n.act += 1
            n.vec = n.vec2

        def before_scatter():
            with nc.Block() as block:
                @block.vector
                def _(dve):
                    run = chain(dve, "vec")
                    run(nc.vector.tensor_copy(spare, feats))
                    run(nc.vector.tensor_tensor(acc[:, :, 0:F], feats, feats, ALU.mult))
                    run(nc.vector.tensor_reduce(col[:, 0, :], acc[:, :, 0:F], AX.X, ALU.add))
                    n.vec = run.count
                    dve.wait_ge(s.act, n.act + 1)
                    run(nc.vector.tensor_scalar(col[:, 1, :], col[:, 1, :], 1e-12, None, ALU.max))
                    run(nc.vector.reciprocal(col[:, 2, :], col[:, 1, :]))
                    run(nc.vector.tensor_tensor(feats, feats, all_lanes(col[:, 2, :], F), ALU.mult))
                    run(nc.vector.memset(xcur[:, :, F:FX], 1.0))
                    n.vec2 = run.count

                @block.scalar
                def _(act):
                    act.wait_ge(s.vec, n.vec)
                    nc.scalar.activation(col[:, 1, :], col[:, 0, :], ACT.Sqrt).then_inc(s.act, 1)
                    nc.scalar.activation(scratch[:, 0:S], w_col[:, :], ACT.Exp, bias=pars[:, 5:6],
                                         scale=pars[:, 0:1]).then_inc(s.act, 1)
                    n.act += 2
            n.vec = n.vec2

        def finish():
            half_blocks = NB // 2
            words = half_blocks * FX
            total = acc[:, :, 0:FX]
            parts = [(t, h) for h in range(2) for t in range(TABLES)]
            with nc.Block() as block:
                @block.sync
                def _(sp):
                    for m, (t, h) in enumerate(parts):
                        if m >= 2:
                            sp.wait_ge(s.finish_used, m - 1)
                        of = d.scattered[t][h * half_blocks * P:(h + 1) * half_blocks * P, :]
                        sp.dma_start(scratch[:, (m % 2) * words:(m % 2 + 1) * words].rearrange("p (b f) -> p b f", f=FX),
                                     of.rearrange("(b p) f -> p b f", p=P)).then_inc(s.finish_in[m % 2], 16)

                @block.vector
                def _(dve):
                    run = chain(dve, "vec")
                    for m, (t, h) in enumerate(parts):
                        dve.wait_ge(s.finish_in[m % 2], 16 * (m // 2 + 1))
                        part = scratch[:, (m % 2) * words:(m % 2 + 1) * words].rearrange("p (b f) -> p b f", f=FX)
                        to = total[:, h * half_blocks:(h + 1) * half_blocks, :]
                        if t == 0:
                            nc.vector.tensor_copy(to, part).then_inc(s.finish_used, 1)
                        else:
                            nc.vector.tensor_tensor(to, to, part, ALU.add).then_inc(s.finish_used, 1)
                        dve.wait_ge(s.finish_used, m + 1)
                    run(nc.vector.scalar_tensor_tensor(total, xcur[:, :, :], pars[:, 3:4], total, ALU.mult, ALU.add))
                    run(nc.vector.tensor_scalar(col[:, 0, :], acc[:, :, F], 1e-16, None, ALU.add))
                    run(nc.vector.reciprocal(col[:, 0, :], col[:, 0, :]))
                    run(nc.vector.tensor_tensor(acc[:, :, 0:F], acc[:, :, 0:F], all_lanes(col[:, 0, :], F), ALU.mult))
                    run(nc.vector.scalar_tensor_tensor(feats, feats, pars[:, 4:5], acc[:, :, 0:F], ALU.mult, ALU.add))
                    run(nc.vector.tensor_tensor(feats, feats, spare, ALU.add))
                    n.vec = run.count
            layer_norm()
            with nc.Block() as block:
                @block.sync
                def _(sp):
                    sp.dma_start(out[0:(NB - 1) * P, :].rearrange("(b p) f -> p b f", p=P),
                                 xcur[:, 0:NB - 1, 0:F]).then_inc(s.stored, 16)
                    sp.dma_start(out[(NB - 1) * P:N, :], xcur[0:last_lanes, NB - 1, 0:F]).then_inc(s.stored, 16)
                    n.stored += 32
                    sp.wait_ge(s.stored, n.stored)

        constants()
        walk()
        sum_by_lane("weighted", 0, FX, x, 0)
        after_weighted_sum()
        layer_norm()
        project(feats, F, w1_sb[:, :], H, "hop1")
        before_hop1()
        sum_by_lane("plain_hist", 1, H, d.hop1, 1)
        between_hops()
        sum_by_lane("plain_dups", 2, H, d.hop2, 2)
        after_hops()
        project(acc[:, :, 0:H], H, w2_sb[:, :], F, "gcn")
        layer_norm()
        before_scores()
        score_walk()
        edge_softmax()
        sum_by_lane("heads", 3, 2 * FX)
        head_means()
        project(heads4[:, :, :, 0:F], P, w_heads[:, :], F, "heads")
        batch_norm()
        layer_norm()
        n.idx = 2 + 2 * 4 * ITS
        before_scatter()
        scatter_walk()
        finish()



_INS = ['x', 'src', 'dst', 'edge_attr_64', 'edge_weight', 'L1_gnn_W1', 'L1_gnn_b1', 'L1_gnn_W2', 'L1_gnn_b2',
        'L2_gnn_W', 'L2_gnn_attn_l', 'L2_gnn_attn_r', 'L2_gnn_bn_gamma', 'L2_gnn_bn_beta', 'L3_gnn_beta', 'L3_gnn_eps']


def laid_out(inputs):
    import numpy as np
    a = {name: np.ascontiguousarray(inputs[name]) for name in _INS}
    n_nodes, n_edges = a['x'].shape[0], a['src'].shape[0]
    tiles, blocks, steps = sizes(n_nodes, n_edges)
    pad_node = blocks * P - 1

    def grown(v, length, fill):
        out = np.full((length,) + v.shape[1:], fill, v.dtype)
        out[:v.shape[0]] = v
        return out

    a['x'] = grown(a['x'], blocks * P, 0)
    a['src'] = grown(a['src'], steps * P, pad_node).reshape(steps, P)
    a['dst'] = grown(a['dst'], steps * P, pad_node).reshape(steps, P)
    a['edge_weight'] = grown(a['edge_weight'], steps * P, 0).reshape(steps, P)
    a['edge_attr_64'] = grown(a['edge_attr_64'], (steps - blocks + 1) * P, 0)
    return a


def kernel(**inputs):
    import numpy as np
    import concourse.bacc as bacc
    from concourse.bass_utils import run_bass_kernel_spmd

    nc = bacc.Bacc("TRN2", target_bir_lowering=False, num_devices=1)
    arrays, args = {}, []
    for name, a in laid_out(inputs).items():
        arrays[f"in_{name}"] = a
        args.append(nc.dram_tensor(f"in_{name}", a.shape, mybir.dt.from_np(a.dtype), kind="ExternalInput").ap())
    shape = tuple(np.asarray(inputs['x']).shape)
    out = nc.dram_tensor("out", shape, F32, kind="ExternalOutput").ap()
    build(nc, *args, out)
    result = run_bass_kernel_spmd(nc, [arrays], core_ids=[0])
    return result.results[0]["out"]
```

```python
from contextlib import ExitStack

import concourse.bass as bass
from concourse import mybir

F32 = mybir.dt.float32
I32 = mybir.dt.int32
I16 = mybir.dt.int16
U32 = mybir.dt.uint32
ALU = mybir.AluOpType
ACT = mybir.ActivationFunctionType
AX = mybir.AxisListType

P = 128
F = 64
FX = F + 1
H = 16
CHUNK = 8
BODY = 32
GROUP = 4
RING = 16
SUMS = 8
TABLES = 8
BIG = 1.0e30


def sizes(n_nodes, n_edges):
    tiles = -(-n_edges // P)
    blocks = -(-n_nodes // P)
    steps = -(-(tiles + blocks - 1) // P) * P
    return tiles, blocks, steps


class Chain:

    def __init__(self, engine, done, start):
        self.engine, self.done, self.count = engine, done, start

    def __call__(self, instruction):
        self.count += 1
        instruction.then_inc(self.done, 1)
        self.engine.wait_ge(self.done, self.count)


class Tables:
    pass


class Semaphores:
    pass


class Reached:
    loaded = stored = vec = vec2 = act = pe = pool = idx = proj = batch = 0


def build(nc, x, src, dst, edge_attr, ew, W1, b1, W2, b2, W, attn_l, attn_r, gamma, bn_beta, beta, eps, out):
    N = out.shape[0]
    NB = x.shape[0] // P
    S = src.shape[0]
    T = edge_attr.shape[0] // P
    NJ = S // P
    ITS = S // BODY
    NPX = (NB + 1) * P
    TABLE_CUTS = min(c for c in range(1, NB + 2)
                     if (NB + 1) % c == 0 and (NB + 1) // c * FX <= CHUNK * P)

    def dram(name, shape, dt=F32):
        return nc.dram_tensor(name, shape, dt).ap()

    d = Tables()
    d.block_of = dram("block_of", [S], I32)
    d.tile_of = dram("tile_of", [S], I32)
    d.lane = dram("lane", [S * P + 2])
    d.src_rows = dram("src_rows", [S, P])
    d.hop1 = dram("hop1", [NB * P, H])
    d.hop2 = dram("hop2", [NB * P, H])
    d.nodes2 = dram("nodes2", [NB * P, FX])
    d.summed_edges = dram("summed_edges", [P, S * FX])
    d.scores = dram("scores", [2, S, P])
    d.weights = dram("weights", [2, S, P])
    d.scattered = [dram(f"scattered{k}", [NPX, FX]) for k in range(TABLES)]
    lane_rows = d.lane[1:1 + S * P].rearrange("(s e) -> s e", e=P)

    ctx = ExitStack()
    with ctx:
        def sb(name, shape, dt=F32):
            return ctx.enter_context(nc.sbuf_tensor(name, shape, dt))

        def sem(name):
            return ctx.enter_context(nc.semaphore(name))

        lanes_free = sb("lanes_free", [P, P])
        lane_id = sb("lane_id", [P, 1])
        earlier = sb("earlier", [P, P])
        ident = sb("ident", [P, P])
        ones = sb("ones", [P, P])
        int_tmp = sb("int_tmp", [P, P], I32)
        xcur = sb("xcur", [P, NB, FX])
        acc = sb("acc", [P, NB, 2 * FX])
        lane_col = sb("lane_col", [P, S + BODY], I16)
        src_col = sb("src_col", [P, S + BODY], I16)
        w_col = sb("w_col", [P, S])
        scatter_col = sb("scatter_col", [P, S + BODY], I16)
        scratch = sb("scratch", [P, 3 * S])
        walk_sb = sb("walk_sb", [P // 2, S], I32)
        idx = sb("idx", [P, BODY], U32)
        rows = sb("rows", [P, RING, FX])
        side = sb("side", [P, RING, FX])
        onehot = sb("onehot", [P, 2 * GROUP, P])
        onehot2 = sb("onehot2", [P, 2 * GROUP, P])
        bcast = sb("bcast", [P, 2, 2 * GROUP * P])
        bcast2 = sb("bcast2", [P, 2, 2 * GROUP * P])
        col = sb("col", [P, 6, NB])
        dinv = sb("dinv", [P, NB])
        inv_norm = sb("inv_norm", [P, NB])
        er = sb("er", [P, NB, 2])
        steps_tmp = sb("steps_tmp", [P, 8, max(NJ, 2)])
        steps_int = sb("steps_int", [P, 3, NJ], I32)
        w1_sb = sb("w1_sb", [F, H])
        w2_sb = sb("w2_sb", [H, F])
        w_heads = sb("w_heads", [P, F])
        v_rows = sb("v_rows", [P, 4, F])
        b1_sb = sb("b1_sb", [P, H])
        b2_sb = sb("b2_sb", [P, F])
        bn_sb = sb("bn_sb", [P, 6, F])
        pars = sb("pars", [P, 8])
        earlier_twins = sb("earlier_twins", [P, P])
        mask = sb("mask", [P, 1])
        dots = sb("dots", [P, GROUP, 2, F])
        dot_sums = sb("dot_sums", [P, GROUP, 2])
        carry_out = sb("carry_out", [P, 4])
        edge_val = sb("edge_val", [P, 6, 1])
        zeros = sb("zeros", [P, P])

        hist_lo = onehot2
        hist_hi = bcast[:, :, :].rearrange("p a b -> p (a b)")[:, 0:2 * GROUP * NB].rearrange("p (s n) -> p s n", n=NB)
        bcast_flat = bcast[:, :, :].rearrange("p a b -> p (a b)")
        bcast2_flat = bcast2[:, :, :].rearrange("p a b -> p (a b)")
        reloaded_rows = [rows, side]
        pairs = [flat[:, 0:2 * GROUP * 2 * FX].rearrange("p (s f) -> p s f", s=2 * GROUP)
                 for flat in (bcast_flat, bcast2_flat)]
        proj_in = [bcast_flat[:, r * 7 * P:(r + 1) * 7 * P] for r in range(2)]
        proj_tr = [bcast2_flat[:, r * 7 * P:(r + 1) * 7 * P] for r in range(2)]
        carry = bcast2_flat[0:1, 0:6 * P].rearrange("o (c p) -> o c p", c=6)
        carry_in = bcast2_flat[0:1, 6 * P:6 * P + 4 * (P + 1)].rearrange("o (c p) -> o c p", c=4)
        clear, clear2 = (flat[:, 0:(NB + 1) * FX // TABLE_CUTS] for flat in (bcast_flat, bcast2_flat))
        w_full = bcast2_flat[0:F, 0:2 * F]
        attn_sb = bcast2_flat[0:F, 2 * F:6 * F].rearrange("k (a d) -> k a d", a=2)
        attn_prod = bcast2_flat[0:F, 6 * F:10 * F].rearrange("k (c d) -> k c d", c=4)
        attn_vb = bcast2_flat[0:F, 10 * F:18 * F].rearrange("k (c p) -> k c p", c=4)
        attn_v = edge_val[0:F, 0:4, 0]
        acc_flat = acc[:, :, :].rearrange("p b f -> p (b f)")

        sums = ctx.enter_context(nc.psum_tensor("sums", [P, SUMS, 256], F32))
        pa = ctx.enter_context(nc.psum_tensor("pa", [P, 1024], F32))
        pb = ctx.enter_context(nc.psum_tensor("pb", [P, 512], F32))
        hist = ctx.enter_context(nc.psum_tensor("hist", [P, 512], F32))

        s = Semaphores()
        s.loaded = sem("loaded")
        s.stored = sem("stored")
        s.vec = sem("vec")
        s.act = sem("act")
        s.pe = sem("pe")
        s.pool = sem("pool")
        s.tiles_in = sem("tiles_in")
        s.gathered = [sem(f"gathered{q}") for q in range(RING // GROUP)]
        s.idx_filled = sem("idx_filled")
        s.weighted = sem("weighted")
        s.matmuls = sem("matmuls")
        s.onehots = sem("onehots")
        s.adds = sem("adds")
        s.hist_ready = sem("hist_ready")
        s.hist_used = sem("hist_used")
        s.src_loaded = [sem(f"src_loaded{h}") for h in range(2)]
        s.dup_counted = sem("dup_counted")
        s.lane_loaded = [sem(f"lane_loaded{h}") for h in range(2)]
        s.bond_loaded = [sem(f"bond_loaded{q}") for q in range(RING // GROUP)]
        s.edge_sums = sem("edge_sums")
        s.er_ready = sem("er_ready")
        s.lane_onehots = sem("lane_onehots")
        s.scored = sem("scored")
        s.spilled = [sem(f"spilled{h}") for h in range(2)]
        s.reloaded = [sem(f"reloaded{c}") for c in range(BODY // CHUNK)]
        s.scaled = sem("scaled")
        s.scaled2 = sem("scaled2")
        s.equal_ready = sem("equal_ready")
        s.spread = sem("spread")
        s.values_ready = sem("values_ready")
        s.cleared = sem("cleared")
        s.merged = sem("merged")
        s.merged_out = sem("merged_out")
        s.scatter_done = [sem(f"scatter_done{k}") for k in range(TABLES)]
        s.batch_t = sem("batch_t")
        s.batch_copied = sem("batch_copied")
        s.proj_in = sem("proj_in_ready")
        s.proj_t = sem("proj_t")
        s.proj_copied = sem("proj_copied")
        s.proj_mm = sem("proj_mm")
        s.finish_used = sem("finish_used")
        s.finish_in = [sem(f"finish_in{h}") for h in range(2)]
        s.proj_out = sem("proj_out")
        n = Reached()

        def load(eng, to, of, slow=False):
            n.loaded += 16
            eng.dma_start(to, of, allow_slow_non_contiguous=slow).then_inc(s.loaded, 16)

        def chain(eng, name):
            return {"vec": Chain(eng, s.vec, n.vec), "act": Chain(eng, s.act, n.act),
                    "pe": Chain(eng, s.pe, n.pe), "pool": Chain(eng, s.pool, n.pool)}[name]

        def all_lanes(ap, width):
            return ap.unsqueeze(2).to_broadcast([P, NB, width])

        def constants():
            with nc.Block() as block:
                @block.sync
                def _(sp):
                    load(sp, xcur[:, :, 0:F], x.rearrange("(b p) f -> p b f", p=P))
                    load(sp, w1_sb[:, :], W1)
                    load(sp, w2_sb[:, :], W2)
                    load(sp, w_full[:, :], W)
                    load(sp, w_heads[0:F, :], W[:, 0:F])
                    load(sp, w_heads[F:P, :], W[:, F:2 * F])
                    load(sp, attn_sb[:, 0, :], attn_l.rearrange("h d -> (h d)").partition_broadcast(F))
                    load(sp, attn_sb[:, 1, :], attn_r.rearrange("h d -> (h d)").partition_broadcast(F))
                    load(sp, b1_sb[:, :], b1.partition_broadcast(P))
                    load(sp, b2_sb[:, :], b2.partition_broadcast(P))
                    load(sp, bn_sb[:, 0, :], gamma.partition_broadcast(P))
                    load(sp, bn_sb[:, 1, :], bn_beta.partition_broadcast(P))
                    load(sp, pars[:, 0:1], beta.partition_broadcast(P))
                    load(sp, pars[:, 1:2], eps.partition_broadcast(P))
                    load(sp, steps_int[:, 0, :], dst[:, P - 1:P].rearrange("(p j) e -> p (j e)", j=NJ), slow=True)
                    sp.wait_ge(s.loaded, n.loaded)

                @block.gpsimd
                def _(pool):
                    run = chain(pool, "pool")
                    run(nc.gpsimd.iota(int_tmp[:, :], [[1, P]], base=0, channel_multiplier=0))
                    run(nc.gpsimd.tensor_copy(lanes_free[:, :], int_tmp[:, :]))
                    run(nc.gpsimd.iota(int_tmp[:, 0:1], [[1, 1]], base=0, channel_multiplier=1))
                    run(nc.gpsimd.tensor_copy(lane_id[:, :], int_tmp[:, 0:1]))
                    run(nc.gpsimd.iota(int_tmp[:, 0:NJ], [[1, NJ]], base=0, channel_multiplier=NJ))
                    run(nc.gpsimd.tensor_copy(steps_tmp[:, 0, 0:NJ], int_tmp[:, 0:NJ]))
                    run(nc.gpsimd.iota(int_tmp[:, 0:NJ], [[P, NJ]], base=0, channel_multiplier=1))
                    run(nc.gpsimd.tensor_copy(steps_tmp[:, 1, 0:NJ], int_tmp[:, 0:NJ]))
                    n.pool = run.count

                @block.vector
                def _(dve):
                    run = chain(dve, "vec")
                    dve.sem_inc(s.proj_out, 2)
                    run(nc.vector.memset(ones[:, :], 1.0))
                    run(nc.vector.memset(acc[:, :, :], 0.0))
                    run(nc.vector.memset(side[:, :, F:FX], 1.0))
                    run(nc.vector.memset(xcur[:, :, F:FX], 1.0))
                    run(nc.vector.memset(zeros[:, :], 0.0))
                    dve.wait_ge(s.pool, n.pool)
                    run(nc.vector.tensor_scalar(ident[:, :], lanes_free[:, :], lane_id[:, 0:1], None, ALU.is_equal))
                    run(nc.vector.tensor_scalar(earlier[:, :], lanes_free[:, :], lane_id[:, 0:1], None, ALU.is_lt))
                    dve.wait_ge(s.loaded, n.loaded)
                    run(nc.vector.tensor_scalar(pars[:, 5:6], pars[:, 0:1], -1.0, None, ALU.mult))
                    run(nc.vector.tensor_tensor(pars[:, 2:3], pars[:, 0:1], pars[:, 5:6], ALU.max))
                    run(nc.vector.tensor_scalar(pars[:, 5:6], pars[:, 2:3], -1.0, None, ALU.mult))
                    run(nc.vector.tensor_tensor(pars[:, 3:4], pars[:, 0:1], pars[:, 5:6], ALU.add))
                    run(nc.vector.tensor_scalar(pars[:, 4:5], pars[:, 1:2], 1.0, None, ALU.add))
                    run(nc.vector.tensor_scalar(w_heads[:, :], w_heads[:, :], 0.5, None, ALU.mult))
                    for side_ in range(2):
                        run(nc.vector.tensor_tensor(
                            attn_prod[:, 2 * side_:2 * side_ + 2, :].rearrange("k c d -> k (c d)"),
                            w_full[:, :], attn_sb[:, side_, :], ALU.mult))
                    run(nc.vector.tensor_reduce(attn_v, attn_prod[:, :, :], AX.X, ALU.add))
                    run(nc.vector.tensor_copy(attn_vb, attn_v.unsqueeze(2).to_broadcast([F, 4, P])))
                    n.vec = run.count

                @block.tensor
                def _(pe):
                    run = chain(pe, "pe")
                    pe.sem_inc(s.proj_t, 2)
                    pe.sem_inc(s.proj_mm, 2)
                    pe.wait_ge(s.vec, n.vec)
                    for c in range(4):
                        run(nc.tensor.matmul(pb[:, F * c:F * c + F], attn_vb[:, c, :], ident[0:F, 0:F],
                                             start=True, stop=True))
                    n.pe = run.count

                @block.scalar
                def _(act):
                    run = chain(act, "act")
                    act.wait_ge(s.vec, n.vec)
                    run(nc.scalar.activation(pars[:, 3:4], pars[:, 3:4], ACT.Exp))
                    act.wait_ge(s.pe, n.pe)
                    run(nc.scalar.copy(v_rows[:, :, :].rearrange("p c f -> p (c f)"), pb[:, 0:4 * F]))
                    n.act = run.count

        def walk():
            src_i = scratch[:, 0:S].bitcast(I32)
            dst_i = scratch[:, S:2 * S].bitcast(I32)
            tile, step, block_at_end, end, tiles_before, of_block, first_node, end_lane = (
                steps_tmp[:, c, 0:NJ] for c in range(8))
            end_lanes = acc_flat[:, 0:S].rearrange("p (j e) -> p j e", e=P)
            end_columns = acc_flat[:, S:S + NJ * NJ].rearrange("p (j c) -> p j c", c=NJ)
            ends = acc_flat[:, 2 * S:2 * S + NJ]
            up_to = acc_flat[:, 2 * S + NJ:2 * S + 2 * NJ]
            later = bcast_flat[:, 0:P]
            with nc.Block() as block:
                @block.vector
                def _(dve):
                    run = chain(dve, "vec")
                    run(nc.vector.tensor_scalar(steps_int[:, 1, :], steps_int[:, 0, :], 7, None, ALU.arith_shift_right))
                    run(nc.vector.tensor_copy(block_at_end, steps_int[:, 1, :]))
                    run(nc.vector.tensor_tensor(end, block_at_end, tile, ALU.add))
                    run(nc.vector.tensor_copy(steps_int[:, 1, :], end))
                    run(nc.vector.tensor_scalar(steps_int[:, 2, :], steps_int[:, 1, :], 7, None, ALU.arith_shift_right))
                    run(nc.vector.tensor_copy(of_block, steps_int[:, 2, :]))
                    run(nc.vector.scalar_tensor_tensor(end_lane, of_block, -float(P), end, ALU.mult, ALU.add))
                    run(nc.vector.tensor_tensor(
                        end_lanes, lanes_free[:, :].unsqueeze(1).to_broadcast([P, NJ, P]),
                        end_lane.unsqueeze(2).to_broadcast([P, NJ, P]), ALU.is_equal))
                    run(nc.vector.tensor_tensor(
                        end_columns, lanes_free[:, 0:NJ].unsqueeze(1).to_broadcast([P, NJ, NJ]),
                        of_block.unsqueeze(2).to_broadcast([P, NJ, NJ]), ALU.is_equal))
                    run(nc.vector.tensor_scalar(later, lanes_free[:, :], lane_id[:, 0:1], None, ALU.is_gt))
                    n.vec = run.count

                @block.tensor
                def _(pe):
                    pe.wait_ge(s.vec, n.vec)
                    for j in range(NJ):
                        last = nc.tensor.matmul(hist[:, 0:NJ], end_lanes[:, j, :], end_columns[:, j, :],
                                                start=j == 0, stop=j == NJ - 1)
                    last.then_inc(s.pe, 1)
                    n.pe += 1
            with nc.Block() as block:
                @block.vector
                def _(dve):
                    run = chain(dve, "vec")
                    dve.wait_ge(s.pe, n.pe)
                    run(nc.vector.tensor_copy(ends, hist[:, 0:NJ]))
                    n.vec = run.count

                @block.tensor
                def _(pe):
                    pe.wait_ge(s.vec, n.vec)
                    nc.tensor.matmul(pa[:, 0:NJ], later, ends, start=True, stop=True).then_inc(s.pe, 1)
                    nc.tensor.matmul(pb[:, 0:NJ], ones[:, :], ends, start=True, stop=True).then_inc(s.pe, 1)
                    n.pe += 2
            with nc.Block() as block:
                @block.vector
                def _(dve):
                    run = chain(dve, "vec")
                    dve.wait_ge(s.pe, n.pe)
                    run(nc.vector.tensor_copy(end, pb[:, 0:NJ]))
                    run(nc.vector.tensor_tensor_scan(up_to, zeros[:, 0:NJ], end, 0.0, ALU.add, ALU.add))
                    run(nc.vector.tensor_tensor(tiles_before, up_to, end, ALU.subtract))
                    run(nc.vector.tensor_tensor(tiles_before, tiles_before, pa[:, 0:NJ], ALU.add))
                    run(nc.vector.tensor_tensor(of_block, step, tiles_before,
                                                ALU.subtract))
                    run(nc.vector.tensor_copy(steps_int[:, 1, :], tiles_before))
                    run(nc.vector.tensor_copy(steps_int[:, 2, :], of_block))
                    run(nc.vector.tensor_scalar(first_node, of_block, float(P), None, ALU.mult))
                    n.vec = run.count

                @block.gpsimd
                def _(pool):
                    pool.wait_ge(s.vec, n.vec)
                    for j in range(NJ):
                        for to, of in ((src_i, src), (dst_i, dst), (scratch[:, 2 * S:3 * S], ew)):
                            pool.indirect_dma_start(
                                out=to[:, j * P:(j + 1) * P], out_offset=None, in_=of[:, :],
                                in_offset=bass.IndirectOffsetOnAxis(ap=steps_int[:, 1, j:j + 1].bitcast(U32), axis=0),
                            ).then_inc(s.tiles_in, 16)
                    pool.wait_ge(s.tiles_in, 3 * NJ * 16)

                @block.sync
                def _(sp):
                    sp.wait_ge(s.vec, n.vec)
                    for of_step, numbers in ((d.tile_of, steps_int[:, 1, :]), (d.block_of, steps_int[:, 2, :])):
                        sp.dma_start(of_step.rearrange("(j p) -> p j", p=P), numbers,
                                     allow_slow_non_contiguous=True).then_inc(s.stored, 16)
                    n.stored += 32
                    sp.wait_ge(s.stored, n.stored)
            with nc.Block() as block:
                tables = ((0, src_col), (1, lane_col), (2, w_col))
                batches = [(j, min(4, NJ - j)) for j in range(0, NJ, 4)]
                start_v = n.vec

                @block.vector
                def _(dve):
                    run = chain(dve, "vec")
                    run(nc.vector.tensor_copy(scratch[:, 0:S], src_i))
                    for j in range(NJ):
                        cut = scratch[:, S + j * P:S + (j + 1) * P]
                        run(nc.vector.tensor_scalar(cut, cut.bitcast(I32), steps_tmp[:, 6, j:j + 1], None,
                                                    ALU.subtract))
                    run(nc.vector.memset(edge_val[:, 0, :], -BIG))
                    made = 0
                    for t, to in tables:
                        for j, m in batches:
                            made += 1
                            dve.wait_ge(s.batch_t, n.batch + made)
                            half = pa[:, (made % 2) * 512:(made % 2) * 512 + m * P]
                            nc.vector.tensor_copy(to[:, j * P:(j + m) * P], half).then_inc(s.batch_copied, 1)
                    dve.wait_ge(s.batch_copied, n.batch + made)
                    run(nc.vector.tensor_copy(src_col[:, S:S + BODY], src_col[:, 0:BODY]))
                    run(nc.vector.tensor_copy(lane_col[:, S:S + BODY], lane_col[:, 0:BODY]))
                    run(nc.vector.memset(acc[:, :, :], 0.0))
                    n.vec = run.count

                @block.tensor
                def _(pe):
                    pe.wait_ge(s.vec, start_v + 1 + NJ)
                    made = 0
                    for t, _to in tables:
                        for j, m in batches:
                            made += 1
                            if made > 2:
                                pe.wait_ge(s.batch_copied, n.batch + made - 2)
                            for q in range(m):
                                to_word = (made % 2) * 512 + q * P
                                last = nc.tensor.transpose(pa[:, to_word:to_word + P],
                                                           scratch[:, t * S + (j + q) * P:t * S + (j + q + 1) * P],
                                                           ident[:, :])
                            last.then_inc(s.batch_t, 1)

                @block.sync
                def _(sp):
                    load(sp, walk_sb[0:1, :], d.block_of.unsqueeze(0))
                    load(sp, walk_sb[32:33, :], d.tile_of.unsqueeze(0))
                    sp.wait_ge(s.vec, start_v + 2 + NJ)
                    rows_of = scratch[:, 0:2 * S].rearrange("p (t j e) -> p t j e", t=2, e=P)
                    load(sp, d.src_rows.rearrange("(j p) e -> p j e", p=P), rows_of[:, 0])
                    load(sp, lane_rows.rearrange("(j p) e -> p j e", p=P), rows_of[:, 1])
                    load(sp, d.lane[0:1].unsqueeze(0), edge_val[0:1, 0, :])
                    load(sp, d.lane[S * P + 1:S * P + 2].unsqueeze(0), edge_val[0:1, 0, :])
                    sp.wait_ge(s.loaded, n.loaded)
            n.batch += 3 * len(batches)

        CH = max(c for c in range(1, 8) if NB % (2 * c) == 0)
        feats = xcur[:, :, 0:F]
        spare = acc[:, :, FX:FX + F]
        last_lanes = N - (NB - 1) * P

        def layer_norm():
            with nc.Block() as block:
                @block.vector
                def _(dve):
                    run = chain(dve, "vec")
                    run(nc.vector.tensor_reduce(col[:, 0, :], feats, AX.X, ALU.add))
                    run(nc.vector.tensor_scalar(col[:, 0, :], col[:, 0, :], 1.0 / F, None, ALU.mult))
                    run(nc.vector.tensor_tensor(feats, feats, all_lanes(col[:, 0, :], F), ALU.subtract))
                    run(nc.vector.tensor_tensor(spare, feats, feats, ALU.mult))
                    run(nc.vector.tensor_reduce(col[:, 1, :], spare, AX.X, ALU.add))
                    run(nc.vector.tensor_scalar(col[:, 1, :], col[:, 1, :], 1.0 / F, 1e-5, ALU.mult, ALU.add))
                    dve.wait_ge(s.act, n.act + 1)
                    run(nc.vector.reciprocal(col[:, 3, :], col[:, 2, :]))
                    run(nc.vector.tensor_tensor(feats, feats, all_lanes(col[:, 3, :], F), ALU.mult))
                    n.vec = run.count

                @block.scalar
                def _(act):
                    act.wait_ge(s.vec, n.vec - 2)
                    nc.scalar.activation(col[:, 2, :], col[:, 1, :], ACT.Sqrt).then_inc(s.act, 1)
                    n.act += 1

        def project(view, depth, weights, width, kind):
            base = n.proj
            rounds = NB // CH
            n.proj += rounds
            heads = len(view.shape) == 4
            transposed_to = [pa[:, 0:CH * P],
                             sums[:, :, :].rearrange("p s f -> p (s f)")[:, 0:CH * P]]
            result = [pb, hist]
            with nc.Block() as block:
                @block.gpsimd
                def _(pool):
                    with pool.Fori(0, rounds // 2) as i:
                        for r in range(2):
                            pool.wait_ge(s.proj_t, i * 2 + (base + r + 1))
                            at = bass.ds(i * (2 * CH) + r * CH, CH)
                            if heads:
                                to = proj_in[r][:, 0:CH * depth].rearrange("p (b h f) -> p b h f", b=CH, h=2)
                                for h in range(2):
                                    last = nc.gpsimd.tensor_copy(to[:, :, h, :], view[:, at, h, :])
                            else:
                                to = proj_in[r][:, 0:CH * depth].rearrange("p (b f) -> p b f", b=CH)
                                last = nc.gpsimd.tensor_copy(to, view[:, at, :])
                            last.then_inc(s.proj_in, 1)

                @block.tensor
                def _(pe):
                    with pe.Fori(0, rounds // 2) as i:
                        for r in range(2):
                            pe.wait_ge(s.proj_in, i * 2 + (base + r + 1))
                            for c in range(CH):
                                last = nc.tensor.matmul(transposed_to[r][0:depth, c * P:(c + 1) * P],
                                                        proj_in[r][:, c * depth:(c + 1) * depth], ident[:, :],
                                                        start=True, stop=True)
                            last.then_inc(s.proj_t, 1)
                        for r in range(2):
                            pe.wait_ge(s.proj_copied, i * 2 + (base + r + 1))
                            pe.wait_ge(s.proj_out, i * 2 + (base + r + 1))
                            for c in range(CH):
                                last = nc.tensor.matmul(result[r][:, c * width:(c + 1) * width],
                                                        proj_tr[r][0:depth, c * P:(c + 1) * P], weights,
                                                        start=True, stop=True)
                            last.then_inc(s.proj_mm, 1)

                @block.scalar
                def _(act):
                    with act.Fori(0, rounds // 2) as i:
                        for r in range(2):
                            act.wait_ge(s.proj_t, i * 2 + (base + r + 3))
                            act.wait_ge(s.proj_mm, i * 2 + (base + r + 1))
                            nc.scalar.copy(proj_tr[r][0:depth, 0:CH * P],
                                           transposed_to[r][0:depth, :]).then_inc(s.proj_copied, 1)

                @block.vector
                def _(dve):
                    with dve.Fori(0, rounds // 2) as i:
                        for r in range(2):
                            at = bass.ds(i * (2 * CH) + r * CH, CH)
                            got = result[r][:, 0:CH * width].rearrange("p (b f) -> p b f", b=CH)
                            dve.wait_ge(s.proj_mm, i * 2 + (base + r + 3))
                            if kind == "hop1":
                                by = dinv[:, at].unsqueeze(2).to_broadcast([P, CH, width])
                                nc.vector.tensor_tensor(acc[:, at, 0:width], got, by,
                                                        ALU.mult).then_inc(s.proj_out, 1)
                            if kind == "gcn":
                                to = xcur[:, at, 0:F]
                                nc.vector.tensor_tensor(to, to, got, ALU.add).then_inc(s.proj_out, 1)
                            if kind == "heads":
                                nc.vector.tensor_copy(acc[:, at, 0:F], got).then_inc(s.proj_out, 1)

        def fill_idx(act, table, at, half):
            act.activation(idx[:, half * RING:(half + 1) * RING], table[:, at], ACT.Copy).then_inc(s.idx_filled, 1)

        def block_numbers(engine, i, k):
            return nc.values_load_multi_w_load_instructions(
                walk_sb[0:1, bass.ds(i * BODY + k, RING)], engines=[engine], min_val=0, max_val=NB - 1,
                skip_runtime_bounds_check_because="steps less tiles, which lies within the blocks")[1]

        def gathers(block, walk_no, table, width, freed, freed_base):
            @block.gpsimd
            def _(pool):
                filled, free = pool.alloc_register(f"filled{walk_no}"), pool.alloc_register(f"free{walk_no}")
                pool.reg_mov(filled, 2 * walk_no * ITS + 1)
                pool.reg_mov(free, freed_base + GROUP)
                with pool.Fori(0, ITS) as _i:
                    for k in range(BODY):
                        if k % RING == 0:
                            pool.wait_ge(s.idx_filled, filled)
                            pool.reg_add(filled, filled, 1)
                        if k % GROUP == 0:
                            pool.wait_ge(freed, free)
                            pool.reg_add(free, free, GROUP)
                        pool.indirect_dma_start(
                            out=rows[:, k % RING, 0:width], out_offset=None, in_=table,
                            in_offset=bass.IndirectOffsetOnAxis(ap=idx[:, k:k + 1], axis=0),
                        ).then_inc(s.gathered[k % RING // GROUP], 16)

        def gathered_by(walk_no, i, k):
            return i * (2 * 16 * GROUP) + (walk_no * S * 4 + 16 * GROUP * (k // RING + 1))

        def sum_by_lane(kind, agg_no, width, table=None, walk_no=None):
            base = agg_no * S
            with nc.Block() as block:
                if table is not None:
                    gathers(block, walk_no, table, width if kind != "weighted" else F, s.matmuls, base)
                if kind == "heads":
                    @block.gpsimd
                    def _(pool):
                        pool.sem_inc(s.scaled2, BODY)
                        with pool.Fori(0, ITS) as i:
                            for k in range(0, BODY, GROUP):
                                half = k // (2 * GROUP) % 2
                                if k % (2 * GROUP) == 0:
                                    pool.wait_ge(s.reloaded[k // CHUNK], i * 16 + 16)
                                pool.wait_ge(s.matmuls, i * BODY + (base + k + GROUP))
                                for j in range(k, k + GROUP):
                                    nc.gpsimd.tensor_tensor(
                                        pairs[half][:, j % (2 * GROUP), FX:2 * FX],
                                        reloaded_rows[k // RING][:, j % RING, :],
                                        scratch[:, bass.ds(i * BODY + (S + j), 1)].to_broadcast([P, FX]),
                                        ALU.mult).then_inc(s.scaled2, 1)

                @block.scalar
                def _(act):
                    if kind == "heads":
                        act.sem_inc(s.scaled, BODY)
                    if walk_no == 0:
                        for half in range(2):
                            fill_idx(act, src_col, slice(half * RING, (half + 1) * RING), half)
                    with act.Fori(0, ITS) as i:
                        for k in range(0, BODY, GROUP):
                            q = k % RING // GROUP
                            if kind == "weighted":
                                act.wait_ge(s.gathered[q], gathered_by(walk_no, i, k))
                                for j in range(k, k + GROUP):
                                    nc.scalar.activation(side[:, j % RING, 0:F], rows[:, j % RING, 0:F], ACT.Copy,
                                                         scale=w_col[:, bass.ds(i * BODY + j, 1)],
                                                         ).then_inc(s.weighted, 1)
                            if kind == "heads":
                                half = k // (2 * GROUP) % 2
                                if k % (2 * GROUP) == 0:
                                    act.wait_ge(s.reloaded[k // CHUNK], i * 16 + 16)
                                act.wait_ge(s.matmuls, i * BODY + (base + k + GROUP))
                                for j in range(k, k + GROUP):
                                    nc.scalar.activation(
                                        pairs[half][:, j % (2 * GROUP), 0:FX],
                                        reloaded_rows[k // RING][:, j % RING, :], ACT.Copy,
                                        scale=scratch[:, bass.ds(i * BODY + j, 1)]).then_inc(s.scaled, 1)
                            if table is not None and q == RING // GROUP - 1:
                                half = k // RING
                                act.wait_ge(s.matmuls, i * BODY + (RING + base + half * RING + RING))
                                fill_idx(act, src_col, bass.ds(i * BODY + (BODY + half * RING), RING)
                                         , half)

                @block.vector
                def _(dve):
                    def make_onehots(at, slot):
                        nc.vector.tensor_tensor(
                            onehot[:, slot * GROUP:(slot + 1) * GROUP, :],
                            lanes_free[:, :].unsqueeze(1).to_broadcast([P, GROUP, P]),
                            lane_col[:, at].unsqueeze(2).to_broadcast([P, GROUP, P]),
                            ALU.is_equal).then_inc(s.onehots, 1)

                    if agg_no == 0:
                        dve.sem_inc(s.adds, SUMS)
                        make_onehots(slice(0, GROUP), 0)
                    if kind == "plain_hist":
                        nc.vector.memset(clear2, 0.0).then_inc(s.vec, 1)
                        n.vec += 1
                    if kind == "plain_dups":
                        dve.sem_inc(s.dup_counted, RING)
                    if kind == "heads":
                        make_onehots(slice(GROUP, 2 * GROUP), 1)
                    with dve.Fori(0, ITS) as i:
                        for k in range(0, BODY, GROUP):
                            if k % RING == 0:
                                blocks_of = block_numbers(mybir.EngineType.DVE, i, k)
                            if kind != "heads":
                                dve.wait_ge(s.matmuls, i * BODY + (RING + base + k))
                                make_onehots(bass.ds(i * BODY + (k + GROUP), GROUP), (k // GROUP + 1) % 2)
                            slot = k // GROUP % 2
                            if kind == "plain_hist":
                                dve.wait_ge(s.hist_used, i * (BODY // GROUP) + (k // GROUP + 1))
                                lo = hist_lo[:, slot * GROUP:(slot + 1) * GROUP, :]
                                hi = hist_hi[:, slot * GROUP:(slot + 1) * GROUP, :]
                                at = i * BODY + k
                                nc.vector.tensor_tensor(
                                    lo, lanes_free[:, :].unsqueeze(1).to_broadcast([P, GROUP, P]),
                                    scratch[:, bass.ds(at, GROUP)].unsqueeze(2).to_broadcast([P, GROUP, P]),
                                    ALU.is_equal).then_inc(s.hist_ready, 1)
                                for j in range(GROUP):
                                    nc.vector.tensor_scalar(
                                        hi[:, j, :], lanes_free[:, 0:NB], scratch[:, bass.ds(at + (S + j), 1)],
                                        scratch[:, bass.ds(at + (2 * S + j), 1)], ALU.is_equal, ALU.mult,
                                    ).then_inc(s.hist_ready, 1)
                            dve.wait_ge(s.matmuls, i * BODY + (RING + base + k + GROUP))
                            for j in range(k, k + GROUP):
                                if kind == "heads":
                                    made = nc.vector.tensor_tensor(
                                        onehot[:, j % (2 * GROUP), :], lanes_free[:, :],
                                        lane_col[:, bass.ds(i * BODY + (j + 2 * GROUP), 1)].to_broadcast([P, P]),
                                        ALU.is_equal)
                                    if j == k + GROUP - 1:
                                        made.then_inc(s.onehots, 1)
                                dve.wait_ge(s.adds, i * BODY + (SUMS + base + j))
                                to = acc[:, bass.ds(blocks_of[j % RING], 1), 0:width].rearrange("p o f -> p (o f)")
                                nc.vector.tensor_tensor(to, to, sums[:, j % SUMS, 0:width],
                                                        ALU.add).then_inc(s.adds, 1)
                                if kind == "plain_dups":
                                    half = k // (2 * GROUP) % 2
                                    if j % (2 * GROUP) == 0:
                                        dve.wait_ge(s.src_loaded[half], i * 32 + 16 * (k // RING + 1))
                                    m = j % (2 * GROUP)
                                    nc.vector.scalar_tensor_tensor(
                                        earlier_twins[:, :], bcast[:, half, m * P:(m + 1) * P],
                                        src_col[:, bass.ds(i * BODY + j, 1)], earlier[:, :],
                                        ALU.is_equal, ALU.mult,
                                        accum_out=scratch[:, bass.ds(i * BODY + j, 1)]).then_inc(s.dup_counted, 1)
                                    dve.wait_ge(s.dup_counted, i * BODY + (RING + j + 1))

                @block.tensor
                def _(pe):
                    if agg_no == 0:
                        pe.sem_inc(s.matmuls, RING)
                    if kind == "plain_hist":
                        pe.sem_inc(s.hist_used, 2)
                        nc.tensor.matmul(hist[:, 0:NB], zeros[:, 0:P], zeros[:, 0:NB], start=True, stop=False)
                    with pe.Fori(0, ITS) as i:
                        for k in range(0, BODY, GROUP):
                            q = k % RING // GROUP
                            if kind == "weighted":
                                pe.wait_ge(s.weighted, i * BODY + (k + GROUP))
                            elif kind == "heads":
                                pe.wait_ge(s.scaled, i * BODY + (BODY + k + GROUP))
                                pe.wait_ge(s.scaled2, i * BODY + (BODY + k + GROUP))
                            else:
                                pe.wait_ge(s.gathered[q], gathered_by(walk_no, i, k))
                            pe.wait_ge(s.onehots, i * (BODY // GROUP) + (base // GROUP + k // GROUP + 1))
                            pe.wait_ge(s.adds, i * BODY + (SUMS + base + k + GROUP - SUMS))
                            for j in range(k, k + GROUP):
                                if kind == "weighted":
                                    of = side[:, j % RING, :]
                                elif kind == "heads":
                                    of = pairs[k // (2 * GROUP) % 2][:, j % (2 * GROUP), :]
                                else:
                                    of = rows[:, j % RING, 0:width]
                                nc.tensor.matmul(sums[:, j % SUMS, 0:width], onehot[:, j % (2 * GROUP), :], of,
                                                 start=True, stop=True).then_inc(s.matmuls, 1)
                            if kind == "plain_hist":
                                pe.wait_ge(s.hist_ready, i * (5 * BODY // GROUP) + 5 * (k // GROUP + 1))
                                slot = k // GROUP % 2
                                for j in range(slot * GROUP, (slot + 1) * GROUP):
                                    last = nc.tensor.matmul(hist[:, 0:NB], hist_lo[:, j, :], hist_hi[:, j, :],
                                                            start=False, stop=False)
                                last.then_inc(s.hist_used, 1)
                    if kind == "plain_hist":
                        pe.wait_ge(s.hist_used, 2 + S // GROUP)
                        nc.tensor.matmul(hist[:, 0:NB], zeros[:, 0:P], zeros[:, 0:NB], start=False,
                                         stop=True).then_inc(s.hist_used, 1)

                @block.sync
                def _(sp):
                    if kind == "plain_hist":
                        sp.wait_ge(s.vec, n.vec)
                        for t in range(TABLES):
                            for c in range(1, TABLE_CUTS):
                                sp.dma_start(table_cuts(t)[c], clear2).then_inc(s.cleared, 16)
                        sp.wait_ge(s.cleared, TABLES * (TABLE_CUTS - 1) * 16)
                    if kind == "plain_dups":
                        free = sp.alloc_register("src_halves")
                        sp.reg_mov(free, 2 * GROUP)
                        with sp.Fori(0, ITS) as i:
                            for c in range(BODY // (2 * GROUP)):
                                sp.wait_ge(s.dup_counted, free)
                                sp.reg_add(free, free, 2 * GROUP)
                                of = d.src_rows[bass.ds(i * BODY + c * 2 * GROUP, 2 * GROUP), :]
                                sp.dma_start(bcast[:, c % 2, :], of.rearrange("s e -> (s e)").partition_broadcast(P),
                                             ).then_inc(s.src_loaded[c % 2], 16)
                    if kind == "heads":
                        free = sp.alloc_register("sum_halves")
                        sp.reg_mov(free, 2 * GROUP)
                        with sp.Fori(0, ITS) as i:
                            for c in range(BODY // (2 * GROUP)):
                                sp.wait_ge(s.scaled, free)
                                sp.wait_ge(s.scaled2, free)
                                sp.reg_add(free, free, 2 * GROUP)
                                at = i * (BODY * FX) + c * 2 * GROUP * FX
                                half = c % 2
                                sp.dma_start(reloaded_rows[c // 2][:, half * 2 * GROUP:(half + 1) * 2 * GROUP, :]
                                             .rearrange("p s f -> p (s f)"),
                                             d.summed_edges[:, bass.ds(at, 2 * GROUP * FX)],
                                             ).then_inc(s.reloaded[c], 16)

        def table_cuts(t):
            return d.scattered[t].rearrange("(c p b) f -> c p (b f)", c=TABLE_CUTS, p=P)

        CHUNKS = BODY // CHUNK

        def chunk_in(sp, of, to, landed, at):
            sp.dma_start(to, of[bass.ds(at, CHUNK), :].rearrange("s e -> (s e)").partition_broadcast(P)
                         ).then_inc(landed, 16)

        def score_walk():
            walk_no = 3
            with nc.Block() as block:
                gathers(block, walk_no, d.nodes2, FX, s.scored, 0)

                @block.vector
                def _(dve):
                    dve.sem_inc(s.scored, RING)
                    dve.sem_inc(s.lane_onehots, 4)
                    with dve.Fori(0, ITS) as i:
                        for k in range(0, BODY, GROUP):
                            q, g = k % RING // GROUP, k // GROUP
                            half, slot = g // 2 % 2, g % 2
                            ops = i * (4 * BODY // GROUP) + 4 * g
                            if slot == 0:
                                dve.wait_ge(s.lane_loaded[half], i * 32 + 16 * (k // RING + 1))
                            dve.wait_ge(s.er_ready, i * (BODY // GROUP) + (g + 1))
                            nc.vector.tensor_scalar(
                                onehot2[:, slot * GROUP:(slot + 1) * GROUP, :].rearrange("p s e -> p (s e)"),
                                bcast2[:, half, slot * GROUP * P:(slot + 1) * GROUP * P], lane_id[:, 0:1], None,
                                ALU.is_equal).then_inc(s.lane_onehots, 1)
                            places = slice(k % RING, k % RING + GROUP)
                            u = side[:, places, 0:F]
                            dve.wait_ge(s.gathered[q], gathered_by(walk_no, i, k))
                            dve.wait_ge(s.bond_loaded[q], i * (2 * 16 * GROUP) + 16 * GROUP * (k // RING + 1))
                            nc.vector.tensor_tensor(u, u, rows[:, places, 0:F], ALU.add).then_inc(s.edge_sums, 1)
                            at = bass.ds(i * BODY + k, GROUP)
                            nc.vector.tensor_tensor(w_col[:, at], w_col[:, at],
                                                    rows[:, places, F:FX].rearrange("p s o -> p (s o)"),
                                                    ALU.mult).then_inc(s.edge_sums, 1)
                            dve.wait_ge(s.edge_sums, ops + 1)
                            nc.vector.tensor_tensor(
                                dots[:, :, :, :], u.unsqueeze(2).to_broadcast([P, GROUP, 2, F]),
                                v_rows[:, 0:2, :].unsqueeze(1).to_broadcast([P, GROUP, 2, F]),
                                ALU.mult).then_inc(s.edge_sums, 1)
                            dve.wait_ge(s.edge_sums, ops + 3)
                            nc.vector.tensor_reduce(dot_sums[:, :, :], dots[:, :, :, :], AX.X,
                                                    ALU.add).then_inc(s.edge_sums, 1)
                            dve.wait_ge(s.edge_sums, ops + 4)
                            dve.wait_ge(s.er_ready, i * (BODY // GROUP) + (g + 3))
                            nc.vector.tensor_tensor(
                                scratch[:, bass.ds(i * (2 * BODY) + 2 * k, 2 * GROUP)],
                                dot_sums[:, :, :].rearrange("p s h -> p (s h)"),
                                pa[:, slot * 512:slot * 512 + 2 * GROUP], ALU.add).then_inc(s.scored, GROUP)

                @block.tensor
                def _(pe):
                    pe.sem_inc(s.er_ready, 2)
                    with pe.Fori(0, ITS) as i:
                        for k in range(0, BODY, GROUP):
                            g, slot = k // GROUP, k // GROUP % 2
                            if k % RING == 0:
                                blocks_of = block_numbers(mybir.EngineType.PE, i, k)
                            pe.wait_ge(s.lane_onehots, i * (BODY // GROUP) + (4 + g + 1))
                            pe.wait_ge(s.scored, i * BODY + (k + 3 * GROUP))
                            for j in range(GROUP):
                                at = slot * 512 + 2 * j
                                last = nc.tensor.matmul(
                                    pa[:, at:at + 2], onehot2[:, slot * GROUP + j, :],
                                    er[:, bass.ds(blocks_of[(k + j) % RING], 1), :].rearrange("p o h -> p (o h)"),
                                    start=True, stop=True)
                            last.then_inc(s.er_ready, 1)

                @block.sync
                def _(sp):
                    lanes_free_at, places_free_at = sp.alloc_register("lanes_at"), sp.alloc_register("places_at")
                    sp.reg_mov(lanes_free_at, 2)
                    sp.reg_mov(places_free_at, 16)
                    with sp.Fori(0, ITS) as i:
                        for c in range(CHUNKS):
                            if c % 2 == 0:
                                tiles_of = nc.values_load_multi_w_load_instructions(
                                    walk_sb[32:33, bass.ds(i * BODY + c * CHUNK, RING)],
                                    engines=[mybir.EngineType.SP], min_val=0, max_val=T - 1,
                                    skip_runtime_bounds_check_because="a count of tiles, which lies within them")[1]
                            sp.wait_ge(s.lane_onehots, lanes_free_at)
                            sp.reg_add(lanes_free_at, lanes_free_at, 2)
                            chunk_in(sp, lane_rows, bcast2[:, c % 2, :], s.lane_loaded[c % 2], i * BODY + c * CHUNK)
                            sp.wait_ge(s.spilled[c % 2], places_free_at)
                            if c % 2 == 1:
                                sp.reg_add(places_free_at, places_free_at, 16)
                            for j in range(c * CHUNK, (c + 1) * CHUNK):
                                sp.dma_start(side[:, j % RING, 0:F],
                                             edge_attr[bass.ds(tiles_of[j % RING] * P, P), :],
                                             ).then_inc(s.bond_loaded[j % RING // GROUP], 16)

                @block.scalar
                def _(act):
                    for half in range(2):
                        act.sem_inc(s.spilled[half], 16)
                    with act.Fori(0, ITS) as i:
                        for c in range(CHUNKS):
                            half = c % 2
                            act.wait_ge(s.scored, i * BODY + (RING + (c + 1) * CHUNK))
                            act.dma_start(d.summed_edges[:, bass.ds(i * (BODY * FX) + c * CHUNK * FX, CHUNK * FX)],
                                          side[:, half * CHUNK:(half + 1) * CHUNK, :].rearrange("p s f -> p (s f)"),
                                          ).then_inc(s.spilled[half], 16)
                            if half == 1:
                                fill_idx(act, src_col, bass.ds(i * BODY + (BODY + (c // 2) * RING), RING), c // 2)
                    for half in range(2):
                        act.wait_ge(s.spilled[half], 16 + S // CHUNK // 2 * 16)

        batches4 = [(j, min(4, NJ - j)) for j in range(0, NJ, 4)]

        def transposed(block, sources, targets):
            base = n.batch
            n.batch += len(sources) * len(batches4)

            def on_pe(pe):
                made = base
                for source in sources:
                    for j, m in batches4:
                        made += 1
                        if made > base + 2:
                            pe.wait_ge(s.batch_copied, made - 2)
                        for q in range(m):
                            last = nc.tensor.transpose(pa[:, (made % 2) * 512 + q * P:(made % 2) * 512 + (q + 1) * P],
                                                       source(j + q), ident[:, :])
                        last.then_inc(s.batch_t, 1)

            def on_dve(dve):
                made = base
                for to in targets:
                    for j, m in batches4:
                        made += 1
                        dve.wait_ge(s.batch_t, made)
                        nc.vector.tensor_copy(to[:, j * P:(j + m) * P],
                                              pa[:, (made % 2) * 512:(made % 2) * 512 + m * P],
                                              ).then_inc(s.batch_copied, 1)
                dve.wait_ge(s.batch_copied, made)
            return on_pe, on_dve

        def edge_softmax():
            raw = scratch[:, 0:2 * S].rearrange("p (s h) -> p s h", h=2)
            by_row = [acc_flat[:, h * S:(h + 1) * S] for h in range(2)]
            score = [scratch[:, h * S:(h + 1) * S] for h in range(2)]
            lanes_x = acc_flat[:, 0:S + 2]
            new_seg = acc_flat[:, S + 2:2 * S + 3]
            fwd = acc_flat[:, 2 * S + 3:3 * S + 3]
            bwd = scratch[:, 2 * S:3 * S]

            with nc.Block() as block:
                on_pe, on_dve = transposed(block, [lambda j, h=h: raw[:, j * P:(j + 1) * P, h] for h in range(2)],
                                           by_row)

                @block.vector
                def _(dve):
                    run = chain(dve, "vec")
                    run(nc.vector.scalar_tensor_tensor(scratch[:, 0:2 * S], scratch[:, 0:2 * S], 0.2,
                                                       scratch[:, 0:2 * S], ALU.mult, ALU.max))
                    n.vec = run.count
                    on_dve(dve)
                    run(nc.vector.memset(carry_in[:, :, :], -BIG))
                    n.vec = run.count

                @block.tensor
                def _(pe):
                    pe.wait_ge(s.vec, n.vec - 1)
                    on_pe(pe)

                @block.gpsimd
                def _(pool):
                    nc.gpsimd.memset(clear, 0.0).then_inc(s.pool, 1)
                    n.pool += 1
                    pool.wait_ge(s.pool, n.pool)
                    for t in range(TABLES):
                        pool.dma_start(table_cuts(t)[0], clear).then_inc(s.scatter_done[t], 16)
                    for t in range(TABLES):
                        pool.wait_ge(s.scatter_done[t], 16)

                @block.sync
                def _(sp):
                    sp.wait_ge(s.batch_copied, n.batch)
                    for h in range(2):
                        sp.dma_start(d.scores[h].rearrange("(j p) e -> p j e", p=P),
                                     by_row[h].rearrange("p (j e) -> p j e", e=P)).then_inc(s.stored, 16)
                    n.stored += 32
                    sp.wait_ge(s.stored, n.stored)
                    for h in range(2):
                        load(sp, score[h], d.scores[h].rearrange("(p j) e -> p (j e)", p=P))
                    load(sp, lanes_x, bass.AP(d.lane.tensor, 0, [[S, P], [1, S + 2]]))
                    sp.wait_ge(s.loaded, n.loaded)

            def scans(run, h, first_f, first_b):
                run(nc.vector.tensor_tensor_scan(fwd, new_seg[:, 0:S], score[h], first_f, ALU.add, ALU.max))
                run(nc.vector.tensor_tensor_scan(bwd[:, ::-1], new_seg[:, S:0:-1], score[h][:, ::-1],
                                                 first_b, ALU.add, ALU.max))

            with nc.Block() as block:
                @block.vector
                def _(dve):
                    run = chain(dve, "vec")
                    run(nc.vector.tensor_tensor(new_seg, lanes_x[:, 0:S + 1], lanes_x[:, 1:S + 2], ALU.not_equal))
                    run(nc.vector.tensor_scalar(new_seg, new_seg, -BIG, None, ALU.mult))
                    run(nc.vector.tensor_reduce(edge_val[:, 4, :], new_seg[:, 0:S], AX.X, ALU.min))
                    run(nc.vector.tensor_reduce(edge_val[:, 5, :], new_seg[:, 1:S + 1], AX.X, ALU.min))
                    for h in range(2):
                        scans(run, h, -BIG, -BIG)
                        run(nc.vector.tensor_copy(edge_val[:, 2 * h, :], fwd[:, S - 1:S]))
                        run(nc.vector.tensor_copy(edge_val[:, 2 * h + 1, :], bwd[:, 0:1]))
                    n.vec = run.count

                @block.tensor
                def _(pe):
                    run = chain(pe, "pe")
                    pe.wait_ge(s.vec, n.vec)
                    for c in range(6):
                        run(nc.tensor.matmul(pa[0:1, c * P:(c + 1) * P], edge_val[:, c, :], ident[:, :],
                                             start=True, stop=True))
                    n.pe = run.count
            with nc.Block() as block:
                @block.vector
                def _(dve):
                    run = chain(dve, "vec")
                    run(nc.vector.tensor_copy(carry[:, :, :].rearrange("o c p -> o (c p)"), pa[0:1, 0:6 * P]))
                    for h in range(2):
                        run(nc.vector.tensor_tensor_scan(carry_in[:, 2 * h, 1:P + 1], carry[:, 4, :],
                                                         carry[:, 2 * h, :], -BIG, ALU.add, ALU.max))
                        run(nc.vector.tensor_tensor_scan(carry_in[:, 2 * h + 1, P - 1::-1], carry[:, 5, ::-1],
                                                         carry[:, 2 * h + 1, ::-1], -BIG, ALU.add, ALU.max))
                    n.vec = run.count

                @block.tensor
                def _(pe):
                    run = chain(pe, "pe")
                    pe.wait_ge(s.vec, n.vec)
                    for c in range(4):
                        run(nc.tensor.matmul(pb[:, c:c + 1], carry_in[:, c, c % 2:c % 2 + P], ones[0:1, 0:1],
                                             start=True, stop=True))
                    n.pe = run.count
            with nc.Block() as block:
                @block.vector
                def _(dve):
                    run = chain(dve, "vec")
                    run(nc.vector.tensor_copy(carry_out[:, :], pb[:, 0:4]))
                    for h in range(2):
                        scans(run, h, carry_out[:, 2 * h:2 * h + 1], carry_out[:, 2 * h + 1:2 * h + 2])
                        run(nc.vector.tensor_tensor(fwd, fwd, bwd, ALU.max))
                        run(nc.vector.tensor_tensor(score[h], score[h], fwd, ALU.subtract))
                    n.vec = run.count

                @block.scalar
                def _(act):
                    run = chain(act, "act")
                    for h in range(2):
                        act.wait_ge(s.vec, n.vec - (4 if h == 0 else 0))
                        run(nc.scalar.activation(score[h], score[h], ACT.Exp))
                    n.act = run.count

                @block.sync
                def _(sp):
                    for h in range(2):
                        sp.wait_ge(s.act, n.act - 1 + h)
                        sp.dma_start(d.weights[h].rearrange("(p j) e -> p (j e)", p=P), score[h]
                                     ).then_inc(s.stored, 16)
                    n.stored += 32
                    sp.wait_ge(s.stored, n.stored)
                    for h in range(2):
                        load(sp, by_row[h].rearrange("p (j e) -> p j e", e=P),
                             d.weights[h].rearrange("(j p) e -> p j e", p=P))
                    sp.wait_ge(s.loaded, n.loaded)
            with nc.Block() as block:
                on_pe, on_dve = transposed(
                    block, [lambda j, h=h: acc_flat[:, h * S + j * P:h * S + (j + 1) * P] for h in range(2)],
                    [scratch[:, h * S:(h + 1) * S] for h in range(2)])

                @block.vector
                def _(dve):
                    run = chain(dve, "vec")
                    on_dve(dve)
                    run(nc.vector.memset(acc[:, :, :], 0.0))
                    n.vec = run.count

                @block.tensor
                def _(pe):
                    on_pe(pe)

        def scatter_walk():
            with nc.Block() as block:
                @block.gpsimd
                def _(pool):
                    filled, ready = pool.alloc_register("filled4"), pool.alloc_register("ready")
                    pool.reg_mov(filled, n.idx + 1)
                    pool.reg_mov(ready, 2 + 1)
                    over = [pool.alloc_register(f"over{t}") for t in range(TABLES)]
                    for t in range(TABLES):
                        pool.reg_mov(over[t], 16)
                    with pool.Fori(0, ITS) as _i:
                        for k in range(BODY):
                            if k % RING == 0:
                                pool.wait_ge(s.idx_filled, filled)
                                pool.reg_add(filled, filled, 1)
                            if k % GROUP == 0:
                                pool.wait_ge(s.merged_out, ready)
                                pool.reg_add(ready, ready, 1)
                            t = k % TABLES
                            pool.wait_ge(s.scatter_done[t], over[t])
                            pool.reg_add(over[t], over[t], 16)
                            pool.indirect_dma_start(
                                out=d.scattered[t], out_offset=bass.IndirectOffsetOnAxis(ap=idx[:, k:k + 1], axis=0),
                                in_=rows[:, k % RING, :], in_offset=None, compute_op=ALU.add,
                            ).then_inc(s.scatter_done[t], 16)
                    for t in range(TABLES):
                        pool.wait_ge(s.scatter_done[t], 16 + 16 * (S // TABLES))

                @block.vector
                def _(dve):
                    dve.sem_inc(s.equal_ready, 4)
                    with dve.Fori(0, ITS) as i:
                        for k in range(0, BODY, GROUP):
                            g, half, slot = k // GROUP, k // CHUNK % 2, k // GROUP % 2
                            if slot == 0:
                                dve.wait_ge(s.lane_loaded[half], i * 32 + (32 * ITS + 16 * (k // RING + 1)))
                                dve.wait_ge(s.src_loaded[half], i * 32 + (32 * ITS + 16 * (k // RING + 1)))
                            dve.wait_ge(s.spread, i * BODY + (k + GROUP))
                            nc.vector.tensor_scalar(
                                onehot2[:, slot * GROUP:(slot + 1) * GROUP, :].rearrange("p s e -> p (s e)"),
                                bcast2[:, half, slot * GROUP * P:(slot + 1) * GROUP * P], lane_id[:, 0:1], None,
                                ALU.is_equal).then_inc(s.lane_onehots, 1)
                            dve.wait_ge(s.merged, i * (BODY // GROUP) + (g + 1))
                            nc.vector.tensor_tensor(
                                onehot[:, slot * GROUP:(slot + 1) * GROUP, :],
                                bcast[:, half, slot * GROUP * P:(slot + 1) * GROUP * P]
                                .rearrange("p (s e) -> p s e", e=P),
                                src_col[:, bass.ds(i * BODY + k, GROUP)].unsqueeze(2).to_broadcast([P, GROUP, P]),
                                ALU.is_equal).then_inc(s.equal_ready, 1)

                @block.tensor
                def _(pe):
                    def merge(i, g):
                        slot = g % 2
                        pe.wait_ge(s.equal_ready, i * (BODY // GROUP) + (4 + g + 1))
                        pe.wait_ge(s.values_ready, i * BODY + (g + 1) * GROUP)
                        pe.wait_ge(s.merged_out, i * (BODY // GROUP) + (g + 1))
                        for j in range(GROUP):
                            last = nc.tensor.matmul(pa[:, slot * 512 + j * FX:slot * 512 + (j + 1) * FX],
                                                    onehot[:, slot * GROUP + j, :],
                                                    side[:, slot * GROUP + j, :], start=True, stop=True)
                        last.then_inc(s.merged, 1)

                    pe.sem_inc(s.merged, 2)
                    pe.sem_inc(s.spread, 2 * GROUP)
                    with pe.Fori(0, ITS) as i:
                        for k in range(0, BODY, GROUP):
                            g, slot = k // GROUP, k // GROUP % 2
                            if k % RING == 0:
                                blocks_of = block_numbers(mybir.EngineType.PE, i, k)
                            pe.wait_ge(s.lane_onehots, i * (BODY // GROUP) + (4 + S // GROUP + g + 1))
                            for j in range(GROUP):
                                nc.tensor.matmul(
                                    sums[:, slot * GROUP + j, 0:FX], onehot2[:, slot * GROUP + j, :],
                                    xcur[:, bass.ds(blocks_of[(k + j) % RING], 1), :].rearrange("p o f -> p (o f)"),
                                    start=True, stop=True).then_inc(s.spread, 1)
                            if g > 0:
                                merge(i, g - 1)
                            if g == BODY // GROUP - 1:
                                merge(i, g)

                @block.scalar
                def _(act):
                    def bring_out(i, k):
                        slot = k // GROUP % 2
                        act.wait_ge(s.merged, i * (BODY // GROUP) + (k // GROUP + 3))
                        for j in range(k, k + GROUP):
                            act.wait_ge(s.scatter_done[j % TABLES],
                                        i * (16 * BODY // TABLES) + 16 * (j // TABLES))
                        nc.scalar.copy(
                            rows[:, k % RING:k % RING + GROUP, :].rearrange("p s f -> p (s f)"),
                            pa[:, slot * 512:slot * 512 + GROUP * FX]).then_inc(s.merged_out, 1)

                    act.sem_inc(s.merged_out, 2)
                    fill_idx(act, scatter_col, slice(0, RING), 0)
                    with act.Fori(0, ITS) as i:
                        for k in range(0, BODY, GROUP):
                            g, slot = k // GROUP, k // GROUP % 2
                            act.wait_ge(s.merged, i * (BODY // GROUP) + (g + 1))
                            act.wait_ge(s.spread, i * BODY + (3 * GROUP + k))
                            for j in range(GROUP):
                                nc.scalar.activation(side[:, slot * GROUP + j, :],
                                                     sums[:, slot * GROUP + j, 0:FX], ACT.Copy,
                                                     scale=scratch[:, bass.ds(i * BODY + (k + j), 1)],
                                                     ).then_inc(s.values_ready, 1)
                            if g > 0:
                                bring_out(i, k - GROUP)
                            if k == BODY - GROUP:
                                bring_out(i, k)
                            if k == RING:
                                fill_idx(act, scatter_col, bass.ds(i * BODY + RING, RING), 1)
                            if k == BODY - GROUP:
                                fill_idx(act, scatter_col, bass.ds(i * BODY + BODY, RING), 0)

                @block.sync
                def _(sp):
                    free = sp.alloc_register("scatter_halves")
                    sp.reg_mov(free, 2)
                    with sp.Fori(0, ITS) as i:
                        for c in range(CHUNKS):
                            sp.wait_ge(s.equal_ready, free)
                            sp.reg_add(free, free, 2)
                            at = i * BODY + c * CHUNK
                            chunk_in(sp, lane_rows, bcast2[:, c % 2, :], s.lane_loaded[c % 2], at)
                            chunk_in(sp, d.src_rows, bcast[:, c % 2, :], s.src_loaded[c % 2], at)

        def after_weighted_sum():
            with nc.Block() as block:
                @block.vector
                def _(dve):
                    run = chain(dve, "vec")
                    run(nc.vector.tensor_tensor(feats, feats, acc[:, :, 0:F], ALU.add))
                    run(nc.vector.tensor_scalar(col[:, 4, :], acc[:, :, F], 1.0, None, ALU.add))
                    run(nc.vector.reciprocal(col[:, 5, :], col[:, 4, :]))
                    n.vec = run.count

                @block.scalar
                def _(act):
                    act.wait_ge(s.vec, n.vec)
                    nc.scalar.activation(dinv[:, :], col[:, 5, :], ACT.Sqrt).then_inc(s.act, 1)
                    n.act += 1

        def before_hop1():
            lo, hi, sq = (scratch[:, t * S:(t + 1) * S] for t in range(3))
            with nc.Block() as block:
                @block.vector
                def _(dve):
                    run = chain(dve, "vec")
                    run(nc.vector.tensor_scalar(hi, lane_col[:, 0:S], -0.5, None, ALU.is_gt))
                    run(nc.vector.tensor_scalar(lo, lane_col[:, 0:S], P - 0.5, None, ALU.is_lt))
                    run(nc.vector.tensor_tensor(lo, lo, hi, ALU.mult))
                    run(nc.vector.tensor_tensor(sq, w_col[:, :], w_col[:, :], ALU.mult))
                    run(nc.vector.tensor_tensor(sq, sq, lo, ALU.mult))
                    run(nc.vector.tensor_copy(lo.bitcast(I32), src_col[:, 0:S]))
                    run(nc.vector.tensor_scalar(hi.bitcast(I32), lo.bitcast(I32), 7, None, ALU.arith_shift_right))
                    run(nc.vector.tensor_copy(hi, hi.bitcast(I32)))
                    run(nc.vector.scalar_tensor_tensor(lo, hi, -float(P), src_col[:, 0:S], ALU.mult, ALU.add))
                    n.vec = run.count

                @block.sync
                def _(sp):
                    sp.dma_start(d.hop1.rearrange("(b p) f -> p b f", p=P), acc[:, :, 0:H]).then_inc(s.stored, 16)
                    n.stored += 16
                    sp.wait_ge(s.stored, n.stored)

        def between_hops():
            with nc.Block() as block:
                @block.vector
                def _(dve):
                    run = chain(dve, "vec")
                    by = all_lanes(dinv[:, :], H)
                    z = acc[:, :, 0:H]
                    run(nc.vector.tensor_tensor(z, z, by, ALU.mult))
                    run(nc.vector.tensor_tensor(z, z, b1_sb[:, :].unsqueeze(1).to_broadcast([P, NB, H]), ALU.add))
                    run(nc.vector.tensor_tensor(z, z, by, ALU.mult))
                    n.vec = run.count
                    dve.wait_ge(s.act, n.act + 1)
                    run(nc.vector.tensor_scalar(col[:, 5, :], col[:, 4, :], 1e-12, None, ALU.max))
                    run(nc.vector.reciprocal(inv_norm[:, :], col[:, 5, :]))
                    n.vec2 = run.count

                @block.scalar
                def _(act):
                    nc.scalar.activation(col[:, 4, :], hist[:, 0:NB], ACT.Sqrt).then_inc(s.act, 1)
                    n.act += 1

                @block.sync
                def _(sp):
                    sp.wait_ge(s.vec, n.vec)
                    sp.dma_start(d.hop2.rearrange("(b p) f -> p b f", p=P), acc[:, :, 0:H]).then_inc(s.stored, 16)
                    n.stored += 16
                    sp.wait_ge(s.stored, n.stored)
            n.vec = n.vec2

        def after_hops():
            with nc.Block() as block:
                @block.vector
                def _(dve):
                    run = chain(dve, "vec")
                    z = acc[:, :, 0:H]
                    run(nc.vector.tensor_tensor(z, z, all_lanes(dinv[:, :], H), ALU.mult))
                    run(nc.vector.tensor_tensor(feats, feats, b2_sb[:, :].unsqueeze(1).to_broadcast([P, NB, F]),
                                                ALU.add))
                    sc, tmp = scratch[:, 0:S], scratch[:, S:2 * S]
                    run(nc.vector.tensor_scalar(mask[:, :], lane_id[:, :], float(NB * P), None, ALU.add))
                    run(nc.vector.tensor_scalar(tmp, src_col[:, 0:S], mask[:, 0:1], None, ALU.subtract))
                    run(nc.vector.scalar_tensor_tensor(sc, sc, 0.0, tmp, ALU.is_equal, ALU.mult))
                    run(nc.vector.tensor_scalar(scatter_col[:, 0:S], sc, mask[:, 0:1], None, ALU.add))
                    run(nc.vector.tensor_copy(scatter_col[:, S:S + BODY], scatter_col[:, 0:BODY]))
                    n.vec = run.count

        def before_scores():
            with nc.Block() as block:
                @block.vector
                def _(dve):
                    run = chain(dve, "vec")
                    run(nc.vector.tensor_copy(xcur[:, :, F], inv_norm[:, :]))
                    n.vec = run.count
                    for h in range(2):
                        run(nc.vector.tensor_tensor(spare, feats,
                                                    v_rows[:, 2 + h, :].unsqueeze(1).to_broadcast([P, NB, F]),
                                                    ALU.mult))
                        run(nc.vector.tensor_reduce(er[:, :, h], spare, AX.X, ALU.add))
                    n.vec2 = run.count

                @block.sync
                def _(sp):
                    sp.wait_ge(s.vec, n.vec)
                    sp.dma_start(d.nodes2.rearrange("(b p) f -> p b f", p=P), xcur[:, :, :]).then_inc(s.stored, 16)
                    n.stored += 16
                    sp.wait_ge(s.stored, n.stored)
            n.vec = n.vec2

        heads4 = acc[:, :, :].rearrange("p b (h f) -> p b h f", h=2)

        def head_means():
            with nc.Block() as block:
                @block.vector
                def _(dve):
                    run = chain(dve, "vec")
                    for h in range(2):
                        run(nc.vector.tensor_scalar(col[:, h, :], heads4[:, :, h, F], 1e-30, None, ALU.max))
                        run(nc.vector.reciprocal(col[:, h, :], col[:, h, :]))
                        run(nc.vector.tensor_tensor(heads4[:, :, h, 0:F], heads4[:, :, h, 0:F],
                                                    all_lanes(col[:, h, :], F), ALU.mult))
                    n.vec = run.count

        def batch_norm():
            hv = acc[:, :, 0:F]
            last_block = acc[:, NB - 1, 0:F]

            def node_sum(view, to):
                with nc.Block() as block:
                    @block.vector
                    def _(dve):
                        run = chain(dve, "vec")
                        run(nc.vector.tensor_reduce(bn_sb[:, 2, :], view.rearrange("p b f -> p f b"), AX.X, ALU.add))
                        n.vec = run.count

                    @block.tensor
                    def _(pe):
                        run = chain(pe, "pe")
                        pe.wait_ge(s.vec, n.vec)
                        run(nc.tensor.matmul(pb[:, 0:F], ones[:, :], bn_sb[:, 2, :], start=True, stop=True))
                        n.pe = run.count
                with nc.Block() as block:
                    @block.vector
                    def _(dve):
                        run = chain(dve, "vec")
                        run(nc.vector.tensor_scalar(to, pb[:, 0:F], 1.0 / N, None, ALU.mult))
                        n.vec = run.count

            def all_nodes(ap):
                return ap.unsqueeze(1).to_broadcast([P, NB, F])

            with nc.Block() as block:
                @block.vector
                def _(dve):
                    run = chain(dve, "vec")
                    run(nc.vector.tensor_scalar(mask[:, :], lane_id[:, :], last_lanes - 0.5, None, ALU.is_lt))
                    run(nc.vector.tensor_scalar(last_block, last_block, mask[:, 0:1], None, ALU.mult))
                    n.vec = run.count
            node_sum(hv, bn_sb[:, 3, :])
            with nc.Block() as block:
                @block.vector
                def _(dve):
                    run = chain(dve, "vec")
                    run(nc.vector.tensor_tensor(hv, hv, all_nodes(bn_sb[:, 3, :]), ALU.subtract))
                    run(nc.vector.tensor_scalar(last_block, last_block, mask[:, 0:1], None, ALU.mult))
                    run(nc.vector.tensor_tensor(spare, hv, hv, ALU.mult))
                    n.vec = run.count
            node_sum(spare, bn_sb[:, 4, :])
            with nc.Block() as block:
                @block.vector
                def _(dve):
                    run = chain(dve, "vec")
                    run(nc.vector.tensor_scalar(bn_sb[:, 4, :], bn_sb[:, 4, :], 1e-5, None, ALU.add))
                    n.vec = run.count
                    dve.wait_ge(s.act, n.act + 1)
                    run(nc.vector.reciprocal(bn_sb[:, 4, :], bn_sb[:, 5, :]))
                    run(nc.vector.tensor_tensor(bn_sb[:, 4, :], bn_sb[:, 4, :], bn_sb[:, 0, :], ALU.mult))
                    run(nc.vector.tensor_tensor(hv, hv, all_nodes(bn_sb[:, 4, :]), ALU.mult))
                    run(nc.vector.tensor_tensor(hv, hv, all_nodes(bn_sb[:, 1, :]), ALU.add))
                    run(nc.vector.scalar_tensor_tensor(feats, hv, 0.0, feats, ALU.max, ALU.add))
                    n.vec2 = run.count

                @block.scalar
                def _(act):
                    act.wait_ge(s.vec, n.vec)
                    nc.scalar.activation(bn_sb[:, 5, :], bn_sb[:, 4, :], ACT.Sqrt).then_inc(s.act, 1)
                    n.act += 1
            n.vec = n.vec2

        def before_scatter():
            with nc.Block() as block:
                @block.vector
                def _(dve):
                    run = chain(dve, "vec")
                    run(nc.vector.tensor_copy(spare, feats))
                    run(nc.vector.tensor_tensor(acc[:, :, 0:F], feats, feats, ALU.mult))
                    run(nc.vector.tensor_reduce(col[:, 0, :], acc[:, :, 0:F], AX.X, ALU.add))
                    n.vec = run.count
                    dve.wait_ge(s.act, n.act + 1)
                    run(nc.vector.tensor_scalar(col[:, 1, :], col[:, 1, :], 1e-12, None, ALU.max))
                    run(nc.vector.reciprocal(col[:, 2, :], col[:, 1, :]))
                    run(nc.vector.tensor_tensor(feats, feats, all_lanes(col[:, 2, :], F), ALU.mult))
                    run(nc.vector.memset(xcur[:, :, F:FX], 1.0))
                    n.vec2 = run.count

                @block.scalar
                def _(act):
                    act.wait_ge(s.vec, n.vec)
                    nc.scalar.activation(col[:, 1, :], col[:, 0, :], ACT.Sqrt).then_inc(s.act, 1)
                    nc.scalar.activation(scratch[:, 0:S], w_col[:, :], ACT.Exp, bias=pars[:, 5:6],
                                         scale=pars[:, 0:1]).then_inc(s.act, 1)
                    n.act += 2
            n.vec = n.vec2

        def finish():
            half_blocks = NB // 2
            words = half_blocks * FX
            total = acc[:, :, 0:FX]
            parts = [(t, h) for h in range(2) for t in range(TABLES)]
            with nc.Block() as block:
                @block.sync
                def _(sp):
                    for m, (t, h) in enumerate(parts):
                        if m >= 2:
                            sp.wait_ge(s.finish_used, m - 1)
                        of = d.scattered[t][h * half_blocks * P:(h + 1) * half_blocks * P, :]
                        to = scratch[:, (m % 2) * words:(m % 2 + 1) * words]
                        sp.dma_start(to.rearrange("p (b f) -> p b f", f=FX),
                                     of.rearrange("(b p) f -> p b f", p=P)).then_inc(s.finish_in[m % 2], 16)

                @block.vector
                def _(dve):
                    run = chain(dve, "vec")
                    for m, (t, h) in enumerate(parts):
                        dve.wait_ge(s.finish_in[m % 2], 16 * (m // 2 + 1))
                        part = scratch[:, (m % 2) * words:(m % 2 + 1) * words].rearrange("p (b f) -> p b f", f=FX)
                        to = total[:, h * half_blocks:(h + 1) * half_blocks, :]
                        if t == 0:
                            nc.vector.tensor_copy(to, part).then_inc(s.finish_used, 1)
                        else:
                            nc.vector.tensor_tensor(to, to, part, ALU.add).then_inc(s.finish_used, 1)
                        dve.wait_ge(s.finish_used, m + 1)
                    run(nc.vector.scalar_tensor_tensor(total, xcur[:, :, :], pars[:, 3:4], total, ALU.mult, ALU.add))
                    run(nc.vector.tensor_scalar(col[:, 0, :], acc[:, :, F], 1e-16, None, ALU.add))
                    run(nc.vector.reciprocal(col[:, 0, :], col[:, 0, :]))
                    run(nc.vector.tensor_tensor(acc[:, :, 0:F], acc[:, :, 0:F], all_lanes(col[:, 0, :], F), ALU.mult))
                    run(nc.vector.scalar_tensor_tensor(feats, feats, pars[:, 4:5], acc[:, :, 0:F], ALU.mult, ALU.add))
                    run(nc.vector.tensor_tensor(feats, feats, spare, ALU.add))
                    n.vec = run.count
            layer_norm()
            with nc.Block() as block:
                @block.sync
                def _(sp):
                    sp.dma_start(out[0:(NB - 1) * P, :].rearrange("(b p) f -> p b f", p=P),
                                 xcur[:, 0:NB - 1, 0:F]).then_inc(s.stored, 16)
                    sp.dma_start(out[(NB - 1) * P:N, :], xcur[0:last_lanes, NB - 1, 0:F]).then_inc(s.stored, 16)
                    n.stored += 32
                    sp.wait_ge(s.stored, n.stored)

        constants()
        walk()
        sum_by_lane("weighted", 0, FX, x, 0)
        after_weighted_sum()
        layer_norm()
        project(feats, F, w1_sb[:, :], H, "hop1")
        before_hop1()
        sum_by_lane("plain_hist", 1, H, d.hop1, 1)
        between_hops()
        sum_by_lane("plain_dups", 2, H, d.hop2, 2)
        after_hops()
        project(acc[:, :, 0:H], H, w2_sb[:, :], F, "gcn")
        layer_norm()
        before_scores()
        score_walk()
        edge_softmax()
        sum_by_lane("heads", 3, 2 * FX)
        head_means()
        project(heads4[:, :, :, 0:F], P, w_heads[:, :], F, "heads")
        batch_norm()
        layer_norm()
        n.idx = 2 + 2 * 4 * ITS
        before_scatter()
        scatter_walk()
        finish()



_INS = ['x', 'src', 'dst', 'edge_attr_64', 'edge_weight', 'L1_gnn_W1', 'L1_gnn_b1', 'L1_gnn_W2', 'L1_gnn_b2',
        'L2_gnn_W', 'L2_gnn_attn_l', 'L2_gnn_attn_r', 'L2_gnn_bn_gamma', 'L2_gnn_bn_beta', 'L3_gnn_beta', 'L3_gnn_eps']


def laid_out(inputs):
    import numpy as np
    a = {name: np.ascontiguousarray(inputs[name]) for name in _INS}
    n_nodes, n_edges = a['x'].shape[0], a['src'].shape[0]
    tiles, blocks, steps = sizes(n_nodes, n_edges)
    pad_node = blocks * P - 1

    def grown(v, length, fill):
        out = np.full((length,) + v.shape[1:], fill, v.dtype)
        out[:v.shape[0]] = v
        return out

    a['x'] = grown(a['x'], blocks * P, 0)
    a['src'] = grown(a['src'], steps * P, pad_node).reshape(steps, P)
    a['dst'] = grown(a['dst'], steps * P, pad_node).reshape(steps, P)
    a['edge_weight'] = grown(a['edge_weight'], steps * P, 0).reshape(steps, P)
    a['edge_attr_64'] = grown(a['edge_attr_64'], (steps - blocks + 1) * P, 0)
    return a


def kernel(**inputs):
    import numpy as np
    import concourse.bacc as bacc
    from concourse.bass_utils import run_bass_kernel_spmd

    nc = bacc.Bacc("TRN2", target_bir_lowering=False, num_devices=1)
    arrays, args = {}, []
    for name, a in laid_out(inputs).items():
        arrays[f"in_{name}"] = a
        args.append(nc.dram_tensor(f"in_{name}", a.shape, mybir.dt.from_np(a.dtype), kind="ExternalInput").ap())
    shape = tuple(np.asarray(inputs['x']).shape)
    out = nc.dram_tensor("out", shape, F32, kind="ExternalOutput").ap()
    build(nc, *args, out)
    result = run_bass_kernel_spmd(nc, [arrays], core_ids=[0])
    return result.results[0]["out"]
```
